# Optimizing a Trainium2 kernel written in Bass

```python
import numpy as np
import jax
import jax.numpy as jnp

def _softmax(x, axis=-1):
    return jax.nn.softmax(x, axis=axis)

def _gelu(x):
    return jax.nn.gelu(x, approximate=True)

def _silu(x):
    return jax.nn.silu(x)

def _sigmoid(x):
    return jax.nn.sigmoid(x)

def _layernorm(x, axis=-1, eps=1e-05):
    m = jnp.mean(x, axis=axis, keepdims=True)
    v = jnp.var(x, axis=axis, keepdims=True)
    return (x - m) / jnp.sqrt(v + eps)

def _scatter_add(tgt, idx, src, axis=0):
    return tgt.at[idx].add(src)

def _segment_sum(src, seg, n):
    return jax.ops.segment_sum(src, seg, n)
kernel_name = 'mk_adaln_ffn_d2_seqx_r4_42d1ac'

def setup_inputs(seed: int=0):
    np.random.seed(seed)
    _w = jnp.asarray

    def _rec_inputs():
        import jax
        import jax.numpy as jnp
        _rk = jax.random.key(seed)
        x = 0.5 + 0.2887 * jax.random.normal(jax.random.fold_in(_rk, 1), (16, 256, 256), jnp.float32)
        _lenS = 256 - jax.random.randint(jax.random.fold_in(_rk, 7), (16,), 0, max(1, 256 // 4) + 1, jnp.int32)
        _lenS2 = 256 - jax.random.randint(jax.random.fold_in(_rk, 8), (16,), 0, max(1, 256 // 4) + 1, jnp.int32)
        condB_zX = jax.random.uniform(jax.random.fold_in(_rk, 11), (16,), jnp.float32, 0.0, 0.983423)
        condB_zY = jax.random.uniform(jax.random.fold_in(_rk, 12), (16,), jnp.float32, 0.0, 0.979075)
        condB_zR = jax.random.uniform(jax.random.fold_in(_rk, 13), (16,), jnp.float32, 0.0, 0.9968)
        itok_B_0_8 = jax.random.randint(jax.random.fold_in(_rk, 14), (16,), 0, 9, jnp.int32)
        return (x, condB_zX, condB_zY, condB_zR, itok_B_0_8)
    x, condB_zX, condB_zY, condB_zR, itok_B_0_8 = _rec_inputs()

    def _L0_cond_setup():
        import jax, jax.numpy as jnp
        import numpy as np
        key = jax.random.key(seed)
        k1, k2, k3, k4 = jax.random.split(key, 4)
        B, H, W = (64, 256, 256)
        return {'y': jax.random.uniform(k1, (B, H, W), dtype=jnp.float32), 'zX': jax.random.uniform(k2, (B, 1), dtype=jnp.float32), 'zY': jax.random.uniform(k3, (B, 1), dtype=jnp.float32), 'zR': jax.random.uniform(k4, (B, 1), dtype=jnp.float32), 'dx': 1, 'dy': 1}
    _L0_cond_all = _L0_cond_setup()
    _L0_cond_in = {k: v for k, v in _L0_cond_all.items() if k in ()}
    del _L0_cond_all

    def _L0_ffn_setup():
        import jax, jax.numpy as jnp
        import numpy as np
        BITS = 8
        LORA_RANK = 16
        LORA_ALPHA = 32
        SCALING = LORA_ALPHA / LORA_RANK

        def fake_quant_weight(w, bits=BITS):
            qmax = 2.0 ** (bits - 1) - 1
            scale = jnp.max(jnp.abs(w)) / qmax
            wq = jnp.clip(jnp.round(w / scale), -qmax - 1, qmax) * scale
            return w + jax.lax.stop_gradient(wq - w)

        def qat_lora_linear(x, W, b, A, B):
            Wq = fake_quant_weight(W)
            base = jnp.einsum('bsi,oi->bso', x, Wq) + b
            lora = jnp.einsum('bsr,or->bso', jnp.einsum('bsi,ri->bsr', x, A), B)
            return base + SCALING * lora
        key = jax.random.key(seed)
        ks = jax.random.split(key, 9)
        d, f = (256, 1024)
        s_in = 1.0 / np.sqrt(d)
        s_ff = 1.0 / np.sqrt(f)
        return {'hidden_states': jax.random.normal(ks[0], (4, 512, d), jnp.float32), 'W_fc': jax.random.normal(ks[1], (f, d), jnp.float32) * s_in, 'b_fc': jnp.zeros((f,), jnp.float32), 'A_fc': jax.random.normal(ks[2], (LORA_RANK, d), jnp.float32) * s_in, 'B_fc': jnp.zeros((f, LORA_RANK), jnp.float32), 'W_proj': jax.random.normal(ks[3], (d, f), jnp.float32) * s_ff, 'b_proj': jnp.zeros((d,), jnp.float32), 'A_proj': jax.random.normal(ks[4], (LORA_RANK, f), jnp.float32) * s_ff, 'B_proj': jnp.zeros((d, LORA_RANK), jnp.float32)}
    _L0_ffn_all = _L0_ffn_setup()
    _L0_ffn_in = {k: v for k, v in _L0_ffn_all.items() if k in ('W_fc', 'b_fc', 'A_fc', 'B_fc', 'W_proj', 'b_proj', 'A_proj', 'B_proj')}
    del _L0_ffn_all

    def _L1_cond_setup():
        import jax, jax.numpy as jnp
        import numpy as np
        LN_EPS = 1e-05
        key = jax.random.key(seed)
        ks = jax.random.split(key, 8)
        B, S, H, A, L = (32, 512, 256, 64, 10)
        return {'hidden_states': jax.random.normal(ks[0], (B, S, H), dtype=jnp.float32), 'language_ids': jax.random.randint(ks[1], (B,), 0, L, dtype=jnp.int64), 'W1': jax.random.normal(ks[2], (L, H, A), dtype=jnp.float32) * (1.0 / np.sqrt(H)), 'b1': jnp.zeros((L, A), dtype=jnp.float32), 'W2': jax.random.normal(ks[3], (L, A, H), dtype=jnp.float32) * (1.0 / np.sqrt(A)), 'b2': jnp.zeros((L, H), dtype=jnp.float32), 'gamma': jnp.ones((L, H), dtype=jnp.float32), 'beta': jnp.zeros((L, H), dtype=jnp.float32)}
    _L1_cond_all = _L1_cond_setup()
    _L1_cond_in = {k: v for k, v in _L1_cond_all.items() if k in ('W1', 'b1', 'W2', 'b2', 'gamma', 'beta')}
    del _L1_cond_all

    def _L1_ffn_setup():
        import jax, jax.numpy as jnp
        import numpy as np
        NUM_HEADS = 16
        TOP_K = 2
        key = jax.random.key(seed)
        ks = jax.random.split(key, 5)
        B, S, D, E = (4, 512, 256, 8)
        scale = 0.02
        return {'x': jax.random.normal(ks[0], (B, S, D), dtype=jnp.float32), 'W_qkv': jax.random.normal(ks[1], (D, 3 * D), dtype=jnp.float32) * scale, 'b_qkv': jnp.zeros((3 * D,), dtype=jnp.float32), 'W_gate': jax.random.normal(ks[2], (D, E), dtype=jnp.float32) * scale, 'b_gate': jnp.zeros((E,), dtype=jnp.float32), 'W_experts': jax.random.normal(ks[3], (E, D, D), dtype=jnp.float32) * scale, 'b_experts': jnp.zeros((E, D), dtype=jnp.float32)}
    _L1_ffn_all = _L1_ffn_setup()
    _L1_ffn_in = {k: v for k, v in _L1_ffn_all.items() if k in ('W_qkv', 'b_qkv', 'W_gate', 'b_gate', 'W_experts', 'b_experts')}
    del _L1_ffn_all
    return {'x': x, 'condB_zX': condB_zX, 'condB_zY': condB_zY, 'condB_zR': condB_zR, 'itok_B_0_8': itok_B_0_8, 'L0_ffn_W_fc': _L0_ffn_in['W_fc'], 'L0_ffn_b_fc': _L0_ffn_in['b_fc'], 'L0_ffn_A_fc': _L0_ffn_in['A_fc'], 'L0_ffn_B_fc': _L0_ffn_in['B_fc'], 'L0_ffn_W_proj': _L0_ffn_in['W_proj'], 'L0_ffn_b_proj': _L0_ffn_in['b_proj'], 'L0_ffn_A_proj': _L0_ffn_in['A_proj'], 'L0_ffn_B_proj': _L0_ffn_in['B_proj'], 'L1_cond_W1': _L1_cond_in['W1'], 'L1_cond_b1': _L1_cond_in['b1'], 'L1_cond_W2': _L1_cond_in['W2'], 'L1_cond_b2': _L1_cond_in['b2'], 'L1_cond_gamma': _L1_cond_in['gamma'], 'L1_cond_beta': _L1_cond_in['beta'], 'L1_ffn_W_qkv': _L1_ffn_in['W_qkv'], 'L1_ffn_b_qkv': _L1_ffn_in['b_qkv'], 'L1_ffn_W_gate': _L1_ffn_in['W_gate'], 'L1_ffn_b_gate': _L1_ffn_in['b_gate'], 'L1_ffn_W_experts': _L1_ffn_in['W_experts'], 'L1_ffn_b_experts': _L1_ffn_in['b_experts']}

def reference(x, condB_zX, condB_zY, condB_zR, itok_B_0_8, L0_ffn_W_fc, L0_ffn_b_fc, L0_ffn_A_fc, L0_ffn_B_fc, L0_ffn_W_proj, L0_ffn_b_proj, L0_ffn_A_proj, L0_ffn_B_proj, L1_cond_W1, L1_cond_b1, L1_cond_W2, L1_cond_b2, L1_cond_gamma, L1_cond_beta, L1_ffn_W_qkv, L1_ffn_b_qkv, L1_ffn_W_gate, L1_ffn_b_gate, L1_ffn_W_experts, L1_ffn_b_experts):
    import jax
    import jax.numpy as jnp

    def _L0_cond_ref(y, zX, zY, zR, dx, dy):
        import jax, jax.numpy as jnp
        import numpy as np
        yp_x = jnp.pad(y, ((0, 0), (0, 0), (1, 1)), mode='reflect')
        lap_x = (yp_x[:, :, :-2] - 2.0 * y + yp_x[:, :, 2:]) / (dx * dx)
        yp_y = jnp.pad(y, ((0, 0), (1, 1), (0, 0)), mode='reflect')
        lap_y = (yp_y[:, :-2, :] - 2.0 * y + yp_y[:, 2:, :]) / (dy * dy)
        du_dt = zX[:, :, None] * lap_x + zY[:, :, None] * lap_y + zR[:, :, None] * y * (1.0 - y)
        return du_dt

    def _L0_ffn_ref(hidden_states, W_fc, b_fc, A_fc, B_fc, W_proj, b_proj, A_proj, B_proj):
        import jax, jax.numpy as jnp
        import numpy as np
        BITS = 8
        LORA_RANK = 16
        LORA_ALPHA = 32
        SCALING = LORA_ALPHA / LORA_RANK

        def fake_quant_weight(w, bits=BITS):
            qmax = 2.0 ** (bits - 1) - 1
            scale = jnp.max(jnp.abs(w)) / qmax
            wq = jnp.clip(jnp.round(w / scale), -qmax - 1, qmax) * scale
            return w + jax.lax.stop_gradient(wq - w)

        def qat_lora_linear(x, W, b, A, B):
            Wq = fake_quant_weight(W)
            base = jnp.einsum('bsi,oi->bso', x, Wq) + b
            lora = jnp.einsum('bsr,or->bso', jnp.einsum('bsi,ri->bsr', x, A), B)
            return base + SCALING * lora
        h = qat_lora_linear(hidden_states, W_fc, b_fc, A_fc, B_fc)
        h = jax.nn.gelu(h, approximate=False)
        h = qat_lora_linear(h, W_proj, b_proj, A_proj, B_proj)
        return h

    def _L1_cond_ref(hidden_states, language_ids, W1, b1, W2, b2, gamma, beta):
        import jax, jax.numpy as jnp
        import numpy as np
        LN_EPS = 1e-05
        w1 = W1[language_ids]
        w2 = W2[language_ids]
        h = jnp.einsum('bsh,bha->bsa', hidden_states, w1) + b1[language_ids][:, None, :]
        h = jax.nn.relu(h)
        adapted = jnp.einsum('bsa,bah->bsh', h, w2) + b2[language_ids][:, None, :]
        x = hidden_states + adapted
        mean = jnp.mean(x, axis=-1, keepdims=True)
        var = jnp.mean(jnp.square(x - mean), axis=-1, keepdims=True)
        normed = (x - mean) * jax.lax.rsqrt(var + LN_EPS)
        return normed * gamma[language_ids][:, None, :] + beta[language_ids][:, None, :]

    def _L1_ffn_ref(x, W_qkv, b_qkv, W_gate, b_gate, W_experts, b_experts):
        import jax, jax.numpy as jnp
        import numpy as np
        NUM_HEADS = 16
        TOP_K = 2
        B, S, D = x.shape
        H = NUM_HEADS
        hd = D // H
        E = W_gate.shape[-1]
        qkv = (x @ W_qkv + b_qkv).reshape(B, S, 3, H, hd)
        q, k, v = (qkv[:, :, 0], qkv[:, :, 1], qkv[:, :, 2])
        attn = jnp.einsum('bqhd,bkhd->bhqk', q, k) / jnp.sqrt(jnp.asarray(hd, x.dtype))
        attn = jax.nn.softmax(attn, axis=-1)
        attn_out = jnp.einsum('bhqk,bkhd->bqhd', attn, v).reshape(B, S, D)
        gate = jax.nn.softmax(x @ W_gate + b_gate, axis=-1)
        top_g, top_i = jax.lax.top_k(gate, TOP_K)
        combine = jnp.sum(jax.nn.one_hot(top_i, E, dtype=x.dtype) * top_g[..., None], axis=2)
        expert_out = jnp.einsum('bsd,edf->bsef', x, W_experts) + b_experts
        moe_out = jnp.einsum('bsef,bse->bsf', expert_out, combine)
        return attn_out + moe_out
    x = x + _L0_ffn_ref(_L0_cond_ref(x, condB_zX[:, None], condB_zY[:, None], condB_zR[:, None], 1, 1), L0_ffn_W_fc, L0_ffn_b_fc, L0_ffn_A_fc, L0_ffn_B_fc, L0_ffn_W_proj, L0_ffn_b_proj, L0_ffn_A_proj, L0_ffn_B_proj)
    x = x + _L1_ffn_ref(_L1_cond_ref(x, itok_B_0_8, L1_cond_W1, L1_cond_b1, L1_cond_W2, L1_cond_b2, L1_cond_gamma, L1_cond_beta), L1_ffn_W_qkv, L1_ffn_b_qkv, L1_ffn_W_gate, L1_ffn_b_gate, L1_ffn_W_experts, L1_ffn_b_experts)
    return x

_drawn_inputs = setup_inputs


def setup_inputs(seed=0):
    import zlib

    import numpy as np

    out = dict(_drawn_inputs(seed))
    spreads = {'L0_ffn_b_fc': (0.0, 0.1),
     'L0_ffn_B_fc': (0.0, 0.1),
     'L0_ffn_b_proj': (0.0, 0.1),
     'L0_ffn_B_proj': (0.0, 0.1),
     'L1_cond_b1': (0.0, 0.1),
     'L1_cond_b2': (0.0, 0.1),
     'L1_cond_gamma': (1.0, 0.2),
     'L1_cond_beta': (0.0, 0.1),
     'L1_ffn_b_qkv': (0.0, 0.1),
     'L1_ffn_b_gate': (0.0, 0.1),
     'L1_ffn_b_experts': (0.0, 0.314)}
    factors = {}
    for name, (base, spread) in spreads.items():
        noise = np.random.default_rng([zlib.crc32(name.encode()), seed]).standard_normal(out[name].shape)
        drawn = base * np.exp(spread * noise) if base else spread * noise
        out[name] = jnp.asarray(drawn.astype(out[name].dtype))
    for name, factor in factors.items():
        out[name] = (out[name] * factor).astype(out[name].dtype)
    return out
```

```python
from contextlib import ExitStack

import concourse.bass as bass
from concourse import mybir

ALU = mybir.AluOpType
ACT = mybir.ActivationFunctionType
AX = mybir.AxisListType
F32 = mybir.dt.float32
F32R = mybir.dt.float32r
BF16 = mybir.dt.bfloat16
I32 = mybir.dt.int32

P = 128
B, S, D = 16, 256, 256
F = 1024
H, HD = 16, 16
E = 8
A = 64
R = 16
L = 10

BT = 2
TOK = BT * S
STEPS = B // BT
NT = TOK // P
DC = D // P
FC = F // P
NH = BT * H
NG = NH // 4
VW = HD + 1
QMAX, QMIN = 127.0, -128.0
MAGIC = 1.5 * 2.0**23
LN_EPS = 1e-5
RSQRT_SEED = 1597463007.0

Q_PART = (0, 0, 1, 1, 0, 2, 1, 2)
K_PART = (0, 1, 0, 1, 2, 0, 2, 1)

FFN_UNITS = [("CT", c) for c in range(DC)] + [("FC", f) for f in range(FC)]
MID_UNITS = (
    [("PJ", t) for t in range(NT)]
    + [("XT", c) for c in range(DC)]
    + [("A1", 0)]
    + [("A2", t) for t in range(NT)]
    + [("ZT", c) for c in range(DC)]
)
END_UNITS = [("V", t) for t in range(NT)] + [("QK", m) for m in range(4)] + [("CB", 0)]
for _t in range(NT):
    END_UNITS += [("MB", _t)] + [("ME", 4 * _t + q) for q in range(4)]
UNITS = FFN_UNITS + MID_UNITS + END_UNITS
NU = len(UNITS)
SLOT = {("CT", 0): 1, ("CT", 1): 1, ("PJ", 0): 5, ("PJ", 1): 8, ("PJ", 2): 11, ("PJ", 3): 14,
        ("XT", 0): 17, ("XT", 1): 17, ("A1", 0): 19, ("A2", 0): 21, ("A2", 1): 21, ("A2", 2): 22,
        ("A2", 3): 22, ("ZT", 0): 28, ("ZT", 1): 28}
for _f in range(FC):
    SLOT[("FC", _f)] = 3
SPLIT_SLOT = 4
LN_SLOT = 23
NSLOT = NH + 3


def wait(eng, sem, value):
    if isinstance(value, int) and value <= 0:
        return
    eng.wait_ge(sem, value)


def block_kernel(nc, a, out):
    scr = nc.dram_tensor("qk_parts", (2, 3, D, TOK), BF16, kind="Internal").ap()
    ctx = ExitStack()
    with ctx:
        top = [(nc.sbuf_base + 63) // 64 * 64]

        def sb(name, shape, dt=F32, at=None):
            n = 1
            for s in shape[1:]:
                n *= s
            n = (n * (2 if dt == BF16 else 4) + 63) // 64 * 64
            if at is None:
                at = top[0]
                top[0] += n
            t = nc.alloc_sbuf_tensor_at(name, shape, dt, offset=at)
            return t

        def region(nbytes):
            at = top[0]
            top[0] += nbytes
            return at

        def sem(name):
            return ctx.enter_context(nc.semaphore(name))

        ident = sb("ident", [P, P])
        wfc_h, wfc_l = sb("wfc_h", [P, DC, F], F32R), sb("wfc_l", [P, DC, F], F32R)
        wpj_h, wpj_l = sb("wpj_h", [P, FC, D], F32R), sb("wpj_l", [P, FC, D], F32R)
        wqk_h, wqk_l = sb("wqk_h", [P, DC, 2 * D], F32R), sb("wqk_l", [P, DC, 2 * D], F32R)
        wvg_h, wvg_l = sb("wvg_h", [P, DC, D + E], F32R), sb("wvg_l", [P, DC, D + E], F32R)
        wex_h, wex_l = sb("wex_h", [P, DC, E, D], F32R), sb("wex_l", [P, DC, E, D], F32R)
        bex = sb("bex", [64, D], F32R)
        bias_cols = sb("bias_cols", [P, 12])
        bpj_bc = sb("bpj_bc", [P, D])
        bvg_bc = sb("bvg_bc", [P, D + E])
        rank_row = sb("rank_row", [P, E])
        z_all = sb("z_all", [P, 3, B])
        z_cur = sb("z_cur", [P, 3, BT])

        h_at = region(2 * FC * TOK * 4)
        hid_h = sb("hid_h", [P, FC, TOK], F32R, at=h_at)
        hid_l = sb("hid_l", [P, FC, TOK], F32R, at=h_at + FC * TOK * 4)
        qk_parts = sb("qk_parts_sb", [P, 3, 4, TOK], BF16, at=h_at)
        qk_at = region(2 * H * TOK * 2)
        qs = sb("qs", [P, H, TOK], BF16, at=qk_at)
        ks = sb("ks", [P, H, TOK], BF16, at=qk_at + H * TOK * 2)
        act_h, act_l = sb("act_h", [P, DC, TOK], F32R), sb("act_l", [P, DC, TOK], F32R)
        x = sb("x", [P, NT, D + 2])
        u_at, d_at, t_at = region(4096), region(4096), region(4096)
        up = sb("up", [P, NT, D], at=u_at)
        wraw = sb("wraw", [P, 2, BT, D], at=u_at)
        y = sb("y", [P, NT, D], at=u_at)
        dn = sb("dn", [P, NT, D], at=d_at)
        xb2 = sb("xb2", [P, NT, D], at=d_at)
        lap = sb("lap", [P, NT, D], at=t_at)
        gel = sb("gel", [P, 2, TOK], at=t_at)
        r1 = sb("r1", [P, TOK], at=t_at)
        rs = sb("rs", [P, TOK], F32R, at=t_at + TOK * 4)
        x1 = sb("x1", [P, NT, D])
        acc = sb("acc", [P, NT, D])
        val = sb("val", [P, NT, H * VW + 16])
        p_at, pts_at = region(4096), region(4096)
        prob = sb("prob", [P, 2, 2, S], at=p_at)
        qf = sb("qf", [P, 2, TOK], at=p_at)
        pts = sb("pts", [P, 2, 2, S], at=pts_at)
        ovs = sb("ovs", [P, S])
        tmp = sb("tmp", [P, 2, 4, HD])
        rden = sb("rden", [P, 2, 4, 1])
        nm = sb("nm", [P, 4, 2])
        bc = sb("bc", [P, BT, 3, D])
        w1_h, w1_l = sb("w1_h", [P, BT, DC, P], F32R), sb("w1_l", [P, BT, DC, P], F32R)
        w2_h, w2_l = sb("w2_h", [P, BT, D], F32R), sb("w2_l", [P, BT, D], F32R)
        b1c = sb("b1c", [P, BT])
        st = sb("st", [P, NT, 6])
        mv = sb("mv", [P, NT, 2])
        ve, rsd, rst = sb("ve", [P, NT]), sb("rsd", [P, NT]), sb("rst", [P, NT])
        lg, ge, gt, g2 = (sb(n, [P, NT, E]) for n in ("lg", "ge", "gt", "g2"))
        eq, s1, s2, cmb = (sb(n, [P, NT, E]) for n in ("eq", "s1", "s2", "cmb"))
        gm = sb("gm", [P, NT])
        cs = sb("cs", [P, NT, 64], F32R)
        cbt = sb("cbt", [64, TOK], F32R, at=pts_at)
        amax = sb("amax", [P, 4])
        assert top[0] <= nc.sbuf_base + 212863, top[0]

        wfc_n = sb("wfc_n", [P, FC, D], at=h_at)
        wpj_n = sb("wpj_n", [P, DC, F], at=h_at + 8192)
        tq1 = sb("tq1", [P, 2048], at=h_at + 16384)
        tq2 = sb("tq2", [P, 2048], at=h_at + 24576)
        wex_n = sb("wex_n", [P, DC, E, D], at=qk_at)
        wqkv_n = sb("wqkv_n", [P, DC, 3 * D], at=qk_at + 16384)
        wg_n = sb("wg_n", [P, DC, E], at=qk_at + 22528)
        a_fc = sb("a_fc", [R, D], at=qk_at + 22592)
        b_fcn = sb("b_fcn", [P, FC, R], at=qk_at + 23616)
        b_pjn = sb("b_pjn", [P, DC, R], at=qk_at + 24128)
        bt_pj = sb("bt_pj", [R, D], at=qk_at + 24256)
        bias_rows = sb("bias_rows", [12, P], at=qk_at + 25600)
        bex_raw = sb("bex_raw", [64, D], at=qk_at + 26112)
        bt_fc = sb("bt_fc", [R, F], at=p_at)
        a_pj = sb("a_pj", [R, F], at=pts_at)

        banks = [ctx.enter_context(nc.psum_tensor(f"bank{i}", [P, 512], F32)) for i in range(8)]
        sc = banks[0:3]
        pt = banks[3:5]
        ov = banks[5]
        gen = banks[6:8]

        w_loaded = sem("w_loaded")
        lora_loaded = sem("lora_loaded")
        rest_loaded = sem("rest_loaded")
        bias_loaded = sem("bias_loaded")
        bex_loaded = sem("bex_loaded")
        bex_zeroed = sem("bex_zeroed")
        ident_made = sem("ident_made")
        consts_made = sem("consts_made")
        amax_part = sem("amax_part")
        amax_all = sem("amax_all")
        setup_pe = sem("setup_pe")
        setup_ev = sem("setup_ev")
        eff_ready = sem("eff_ready")
        hi_ready = sem("hi_ready")
        wts_ready = sem("wts_ready")
        v_step = sem("v_step")
        p_step = sem("p_step")

        x_loaded = sem("x_loaded")
        c_ready = sem("c_ready")
        xb_ready = sem("xb_ready")
        ah_ready = sem("ah_ready")
        at_ready = sem("at_ready")
        g_ready = sem("g_ready")
        h_ready = sem("h_ready")
        x1_ready = sem("x1_ready")
        xb2_ready = sem("xb2_ready")
        lang_loaded = sem("lang_loaded")
        lang_split = sem("lang_split")
        r1_ready = sem("r1_ready")
        rs_ready = sem("rs_ready")
        y_ready = sem("y_ready")
        zn_ready = sem("zn_ready")
        z_ready = sem("z_ready")
        v_ready = sem("v_ready")
        qf_ready = sem("qf_ready")
        parts_ready = sem("parts_ready")
        scr_written = sem("scr_written")
        qk_loaded = [sem(f"qk_loaded{b}") for b in range(BT)]
        lg_ready = sem("lg_ready")
        ge_ready = sem("ge_ready")
        comb_ready = sem("comb_ready")
        combt_ready = sem("combt_ready")
        moe_added = sem("moe_added")
        gen_full = sem("gen_full")
        main_step = sem("main_step")
        att_step = sem("att_step")

        s_ready = sem("s_ready")
        nm_ready = sem("nm_ready")
        p_ready = sem("p_ready")
        pt_full = sem("pt_full")
        pts_ready = [sem(f"pts_ready{i}") for i in range(2)]
        pv_done = sem("pv_done")
        ovs_ready = sem("ovs_ready")
        ot_ready = sem("ot_ready")
        ot_used = sem("ot_used")
        att_added = sem("att_added")
        stored = sem("stored")

        settled = {n: sem(f"settled_{n}") for n in ("sp", "pool", "pe", "dve")}

        def settle(eng, name):
            eng.sem_inc(settled[name], 1)

        DONE = {}
        for c in range(DC):
            DONE[("CT", c)] = (at_ready, 3 * DC, c)
            DONE[("XT", c)] = (at_ready, 3 * DC, DC + c)
            DONE[("ZT", c)] = (at_ready, 3 * DC, 2 * DC + c)
        for f in range(FC):
            DONE[("FC", f)] = (g_ready, FC, f)
        for t in range(NT):
            DONE[("PJ", t)] = (x1_ready, NT, t)
            DONE[("A2", t)] = (y_ready, NT, t)
            DONE[("V", t)] = (v_ready, NT, t)
            DONE[("QK", t)] = (qf_ready, 4, t)
            DONE[("MB", t)] = (moe_added, 5 * NT, 5 * t)
            for q in range(4):
                DONE[("ME", 4 * t + q)] = (moe_added, 5 * NT, 5 * t + q + 1)
        DONE[("A1", 0)] = (r1_ready, 1, 0)
        DONE[("CB", 0)] = (combt_ready, 1, 0)

        def full(eng, k, unit):
            eng.wait_ge(gen_full, k * NU + UNITS.index(unit) + 1)

        def signal(ins, unit):
            ins.then_inc(DONE[unit][0], 1)

        def psum(unit):
            return gen[UNITS.index(unit) % 2]

        P_CREDIT, PT_CREDIT, PV_CREDIT = 3, 2, 2

        block = ctx.enter_context(nc.Block())

        @block.sync
        def _(sp):
            sp.dma_start(wfc_n[:], a["L0_ffn_W_fc"].rearrange("(c p) d -> p c d", p=P)).then_inc(w_loaded, 16)
            sp.dma_start(a_fc[:], a["L0_ffn_A_fc"]).then_inc(lora_loaded, 16)
            sp.dma_start(b_fcn[:], a["L0_ffn_B_fc"].rearrange("(c p) r -> p c r", p=P)).then_inc(lora_loaded, 16)
            sp.dma_start(wpj_n[:], a["L0_ffn_W_proj"].rearrange("(c p) f -> p c f", p=P)).then_inc(w_loaded, 16)
            sp.dma_start(a_pj[:], a["L0_ffn_A_proj"]).then_inc(lora_loaded, 16)
            sp.dma_start(b_pjn[:], a["L0_ffn_B_proj"].rearrange("(c p) r -> p c r", p=P)).then_inc(lora_loaded, 16)
            sp.dma_start(bias_rows[0:8, :], a["L0_ffn_b_fc"].rearrange("(c p) -> c p", p=P)).then_inc(bias_loaded, 16)
            sp.dma_start(bias_rows[8:12, :], a["L1_ffn_b_qkv"][0:2 * D].rearrange("(c p) -> c p", p=P)).then_inc(bias_loaded, 16)
            for dst, src in ((bpj_bc[:], a["L0_ffn_b_proj"]), (bvg_bc[:, 0:D], a["L1_ffn_b_qkv"][2 * D:3 * D]),
                             (bvg_bc[:, D:D + E], a["L1_ffn_b_gate"])):
                sp.dma_start(dst, src.partition_broadcast(P)).then_inc(bias_loaded, 16)
            for i, n in enumerate(("condB_zX", "condB_zY", "condB_zR")):
                sp.dma_start(z_all[:, i, :], a[n].partition_broadcast(P)).then_inc(bias_loaded, 16)
            sp.dma_start(wqkv_n[:], a["L1_ffn_W_qkv"].rearrange("(c p) n -> p c n", p=P)).then_inc(rest_loaded, 16)
            sp.dma_start(wg_n[:], a["L1_ffn_W_gate"].rearrange("(c p) n -> p c n", p=P)).then_inc(rest_loaded, 16)
            for c in range(DC):
                sp.dma_start(wex_n[:, c], a["L1_ffn_W_experts"][:, c * P:(c + 1) * P, :].rearrange("e p f -> p e f"))\
                    .then_inc(rest_loaded, 16)
            sp.wait_ge(bex_zeroed, 1)
            for r in (0, 8, 32, 40):
                sp.dma_start(bex_raw[r:r + E, :], a["L1_ffn_b_experts"]).then_inc(bex_loaded, 16)

            def languages(k):
                sp.wait_ge(c_ready, k + 1)
                settle(sp, "sp")
                wait(sp, z_ready, k * NT)
                settle(sp, "sp")
                for b in range(BT):
                    lang = sp.value_load(a["itok_B_0_8"].rearrange("(o n) -> o n", o=1)[:, bass.ds(k * BT + b, 1)],
                                         min_val=0, max_val=L - 1)
                    w1 = a["L1_cond_W1"][bass.ds(lang, 1)].rearrange("l (c p) a -> p (l c) a", p=P)
                    w2 = a["L1_cond_W2"][bass.ds(lang, 1)].rearrange("l a h -> (l a) h")
                    b1 = a["L1_cond_b1"][bass.ds(lang, 1)].rearrange("l a -> a l")
                    for half in range(2):
                        sp.dma_start(wraw[:, 0, b].rearrange("p (c m) -> p c m", c=DC)[:, :, half * A:(half + 1) * A], w1)\
                            .then_inc(lang_loaded, 16)
                        sp.dma_start(wraw[half * A:(half + 1) * A, 1, b], w2).then_inc(lang_loaded, 16)
                        with nc.allow_non_contiguous_dma(reason="one bias for each partition"):
                            sp.dma_start(b1c[half * A:(half + 1) * A, b:b + 1], b1).then_inc(lang_loaded, 16)
                    for i, n in enumerate(("L1_cond_b2", "L1_cond_gamma", "L1_cond_beta")):
                        sp.dma_start(bc[:, b, i], a[n][bass.ds(lang, 1)].rearrange("l h -> (l h)").partition_broadcast(P))\
                            .then_inc(lang_loaded, 16)

            def stores(j):
                for b in range(BT):
                    sp.wait_ge(att_added, j * NG + (b + 1) * NG // BT)
                    settle(sp, "sp")
                    sp.dma_start(out[bass.ds(j * BT + b, 1)].rearrange("b (t p) d -> p (b t) d", p=P),
                                 acc[:, 2 * b:2 * b + 2]).then_inc(stored, 16)

            def stack(k):
                for m in range(4):
                    sp.wait_ge(parts_ready, 4 * k + m + 1)
                    sp.dma_start(scr[m // 2, :, (m % 2) * P:(m % 2 + 1) * P, :].rearrange("s p t -> p s t"),
                                 qk_parts[:, :, m, :]).then_inc(scr_written, 16)
                sp.wait_ge(scr_written, 64 * (k + 1))
                for b in range(BT):
                    for i, (dst, part) in enumerate(((qs, Q_PART), (ks, K_PART))):
                        for c in range(8):
                            sp.dma_start(dst[16 * c:16 * c + 16, :, b * S:(b + 1) * S],
                                         scr[i, part[c], :, b * S:(b + 1) * S].rearrange("(h d) t -> d h t", d=HD))\
                                .then_inc(qk_loaded[b], 16)

            languages(0)
            stack(0)
            with sp.Fori(1, STEPS) as k:
                languages(k)
                stores(k - 1)
                stack(k)
            stores(STEPS - 1)
            sp.wait_ge(stored, 16 * BT * STEPS)

        @block.gpsimd
        def _(pool):
            nc.gpsimd.memset(ident[:], 0.0).then_inc(p_step, 1)
            nc.gpsimd.memset(bex_raw[:], 0.0).then_inc(bex_zeroed, 1)
            pool.wait_ge(p_step, 1)
            nc.gpsimd.affine_select(out=ident[:], in_=ident[:], compare_op=ALU.not_equal, fill=1.0, base=0,
                                    pattern=[[-1, P]], channel_multiplier=1).then_inc(ident_made, 1)
            for e in range(E):
                nc.gpsimd.memset(rank_row[:, e:e + 1], float(E - e))
            nc.gpsimd.memset(val[:], 0.0).then_inc(p_step, 1)
            pool.wait_ge(p_step, 2)
            nc.gpsimd.memset(val[:, :, 0:H * VW].rearrange("p t (h w) -> p t h w", w=VW)[:, :, :, HD:VW], 1.0)
            nc.gpsimd.memset(cs[:].bitcast(F32), 0.0).then_inc(consts_made, 1)
            for i in range(2):
                pool.wait_ge(amax_part, i + 1)
                nc.gpsimd.partition_all_reduce(amax[:, 2 + i:3 + i], amax[:, i:i + 1], P,
                                               bass.bass_isa.ReduceOp.max).then_inc(amax_all, 1)
            pool.wait_ge(bias_loaded, 16 * 8)

            xi = x[:, :, 1:D + 1]
            N_STEP = 14

            def main(k):
                base = 2 + k * N_STEP
                n = [0]

                def link(ins):
                    n[0] += 1
                    ins.then_inc(p_step, 1)
                    pool.wait_ge(p_step, base + n[0])
                    settle(pool, "pool")

                wait(pool, x1_ready, k * NT)
                settle(pool, "pool")
                xs = a["x"][bass.ds(k * BT, BT)]
                for b in range(BT):
                    pool.dma_start(x[:, 2 * b:2 * b + 2, 1:D + 1],
                                   xs[b].rearrange("(t p) d -> p t d", p=P)).then_inc(x_loaded, 16)
                wait(pool, at_ready, k * 3 * DC)
                settle(pool, "pool")
                for b in range(BT):
                    t0, t1 = 2 * b, 2 * b + 1
                    pool.dma_start(up[1:P, t0], xs[b, 0:P - 1]).then_inc(x_loaded, 16)
                    pool.dma_start(up[0:1, t0], xs[b, 1:2]).then_inc(x_loaded, 16)
                    pool.dma_start(up[:, t1], xs[b, P - 1:2 * P - 1]).then_inc(x_loaded, 16)
                    pool.dma_start(dn[:, t0], xs[b, 1:P + 1]).then_inc(x_loaded, 16)
                    pool.dma_start(dn[0:P - 1, t1], xs[b, P + 1:2 * P]).then_inc(x_loaded, 16)
                    pool.dma_start(dn[P - 1:P, t1], xs[b, 2 * P - 2:2 * P - 1]).then_inc(x_loaded, 16)
                nc.gpsimd.tensor_copy(z_cur[:], z_all[:, :, bass.ds(k * BT, BT)])
                pool.wait_ge(x_loaded, 16 * 14 * (k + 1))
                settle(pool, "pool")
                nc.gpsimd.tensor_copy(x[:, :, 0:1], x[:, :, 2:3])
                link(nc.gpsimd.tensor_copy(x[:, :, D + 1:D + 2], x[:, :, D - 1:D]))
                nc.gpsimd.tensor_tensor(dn[:], up[:], dn[:], ALU.add)
                link(nc.gpsimd.tensor_tensor(lap[:], x[:, :, 0:D], x[:, :, 2:D + 2], ALU.add))
                link(nc.gpsimd.tensor_scalar(up[:], xi, -2.0, None, ALU.mult))
                nc.gpsimd.tensor_tensor(dn[:], dn[:], up[:], ALU.add)
                link(nc.gpsimd.tensor_tensor(lap[:], lap[:], up[:], ALU.add))
                for b in range(BT):
                    ts = slice(2 * b, 2 * b + 2)
                    nc.gpsimd.tensor_scalar(dn[:, ts], dn[:, ts], z_cur[:, 1, b:b + 1], None, ALU.mult)
                    ins = nc.gpsimd.tensor_scalar(lap[:, ts], lap[:, ts], z_cur[:, 0, b:b + 1], None, ALU.mult)
                link(ins)
                link(nc.gpsimd.tensor_tensor(lap[:], lap[:], dn[:], ALU.add))
                link(nc.gpsimd.tensor_scalar(dn[:], xi, -1.0, 1.0, ALU.mult, ALU.add))
                link(nc.gpsimd.tensor_tensor(dn[:], dn[:], xi, ALU.mult))
                for b in range(BT):
                    ts = slice(2 * b, 2 * b + 2)
                    ins = nc.gpsimd.tensor_scalar(dn[:, ts], dn[:, ts], z_cur[:, 2, b:b + 1], None, ALU.mult)
                link(ins)
                nc.gpsimd.tensor_tensor(dn[:], lap[:], dn[:], ALU.add).then_inc(c_ready, 1)
                nc.gpsimd.tensor_tensor(xi, xi, bpj_bc[:].unsqueeze(1).to_broadcast([P, NT, D]), ALU.add)\
                    .then_inc(xb_ready, 1)
                pool.wait_ge(lang_loaded, 16 * 18 * (k + 1))
                for t in range(NT):
                    pool.wait_ge(x1_ready, k * NT + t + 1)
                    nc.gpsimd.tensor_tensor(xb2[:, t], x1[:, t], bc[:, t // 2, 0], ALU.add).then_inc(xb2_ready, 1)
                for t in range(NT):
                    pool.wait_ge(zn_ready, k * NT + t + 1)
                    link(nc.gpsimd.tensor_tensor(y[:, t], y[:, t], bc[:, t // 2, 1], ALU.mult))
                    nc.gpsimd.tensor_tensor(y[:, t], y[:, t], bc[:, t // 2, 2], ALU.add).then_inc(z_ready, 1)
                while n[0] < N_STEP:
                    link(nc.gpsimd.tensor_copy(z_cur[:, 0, 0:1], z_cur[:, 0, 0:1]))
                assert n[0] == N_STEP, n[0]

            main(0)
            with pool.Fori(1, STEPS) as k:
                main(k)

        @block.tensor
        def _(pe):
            def mm(o, l, r, start=True, stop=True):
                return pe.matmul(o, l, r, start=start, stop=stop)

            def mm3(o, lh, ll, rh, rl, start, stop):
                mm(o, lh, rh, start, False)
                mm(o, lh, rl, False, False)
                return mm(o, ll, rh, False, stop)

            pe.wait_ge(ident_made, 1)
            pe.wait_ge(lora_loaded, 64)
            job = [0]

            def bank():
                wait(pe, setup_ev, job[0] - 7)
                job[0] += 1
                return banks[(job[0] - 1) % 8]

            for half in range(2):
                o = bank()
                for i in range(4):
                    ins = pe.transpose(o[0:R, i * P:(i + 1) * P], b_fcn[:, 4 * half + i], ident[:])
                ins.then_inc(setup_pe, 1)
            o = bank()
            for c in range(DC):
                ins = pe.transpose(o[0:R, c * P:(c + 1) * P], b_pjn[:, c], ident[:])
            ins.then_inc(setup_pe, 1)
            pe.wait_ge(bias_loaded, 16 * 8)
            o = bank()
            pe.transpose(o[:, 0:12], bias_rows[:], ident[0:12, 0:12]).then_inc(setup_pe, 1)
            pe.wait_ge(setup_ev, 3)
            for f2 in range(FC // 2):
                o = bank()
                for i in range(2):
                    f = 2 * f2 + i
                    ins = mm(o[:, i * D:(i + 1) * D], bt_fc[:, f * P:(f + 1) * P], a_fc[:])
                ins.then_inc(setup_pe, 1)
            for c in range(DC):
                for half in range(2):
                    mm(bank()[:], bt_pj[:, c * P:(c + 1) * P], a_pj[:, half * 512:(half + 1) * 512])\
                        .then_inc(setup_pe, 1)
            pe.wait_ge(eff_ready, 1)
            for c in range(DC):
                for half in range(2):
                    o = bank()
                    for i in range(4):
                        f = 4 * half + i
                        ins = pe.transpose(o[:, i * P:(i + 1) * P], tq2[:, f * D + c * P:f * D + (c + 1) * P], ident[:])
                    ins.then_inc(setup_pe, 1)
            pe.wait_ge(eff_ready, 2)
            for f2 in range(FC // 2):
                o = bank()
                for i in range(2):
                    f = 2 * f2 + i
                    for c in range(DC):
                        ins = pe.transpose(o[:, i * D + c * P:i * D + (c + 1) * P],
                                           tq1[:, c * F + f * P:c * F + (f + 1) * P], ident[:])
                ins.then_inc(setup_pe, 1)
            pe.wait_ge(setup_ev, job[0])
            pe.wait_ge(wts_ready, 1)
            pe.sem_inc(pt_full, PT_CREDIT)
            pe.sem_inc(pv_done, PV_CREDIT)

            def unit(k, u):
                kind, i = u
                at = UNITS.index(u)
                prev = UNITS[at - 2]
                s, n, place = DONE[prev]
                wait(pe, s, (k if at >= 2 else k - 1) * n + place + 1)
                o = psum(u)
                if kind in ("CT", "XT", "ZT"):
                    if kind == "CT":
                        pe.wait_ge(c_ready, k + 1)
                        src = dn
                    elif kind == "XT":
                        pe.wait_ge(x1_ready, (k + 1) * NT)
                        src = x1
                    else:
                        pe.wait_ge(z_ready, (k + 1) * NT)
                        src = y
                    for t in range(NT):
                        ins = pe.transpose(o[:, t * P:(t + 1) * P], src[:, t, i * P:(i + 1) * P], ident[:])
                elif kind == "FC":
                    pe.wait_ge(at_ready, k * 3 * DC + DC)
                    for c in range(DC):
                        w = slice(i * P, (i + 1) * P)
                        ins = mm3(o[:], wfc_h[:, c, w], wfc_l[:, c, w], act_h[:, c], act_l[:, c], c == 0, c == DC - 1)
                elif kind == "PJ":
                    pe.wait_ge(h_ready, (k + 1) * FC)
                    tok = slice(i * P, (i + 1) * P)
                    for f in range(FC):
                        ins = mm3(o[:, 0:D], hid_h[:, f, tok], hid_l[:, f, tok], wpj_h[:, f], wpj_l[:, f],
                                  f == 0, f == FC - 1)
                elif kind == "A1":
                    pe.wait_ge(at_ready, k * 3 * DC + 2 * DC)
                    pe.wait_ge(lang_split, k + 1)
                    for b in range(BT):
                        tok = slice(b * S, (b + 1) * S)
                        for c in range(DC):
                            ins = mm3(o[:, tok], w1_h[:, b, c], w1_l[:, b, c], act_h[:, c, tok], act_l[:, c, tok],
                                      c == 0, c == DC - 1)
                elif kind == "A2":
                    pe.wait_ge(rs_ready, k + 1)
                    tok = slice(i * P, (i + 1) * P)
                    mm(o[:, 0:D], rs[:, tok], w2_h[:, i // 2], True, False)
                    ins = mm(o[:, 0:D], rs[:, tok], w2_l[:, i // 2], False, True)
                elif kind == "V":
                    pe.wait_ge(at_ready, (k + 1) * 3 * DC)
                    tok = slice(i * P, (i + 1) * P)
                    for c in range(DC):
                        ins = mm3(o[:, 0:D + E], act_h[:, c, tok], act_l[:, c, tok], wvg_h[:, c], wvg_l[:, c],
                                  c == 0, c == DC - 1)
                elif kind == "QK":
                    w = slice(i * P, (i + 1) * P)
                    for c in range(DC):
                        ins = mm3(o[:], wqk_h[:, c, w], wqk_l[:, c, w], act_h[:, c], act_l[:, c], c == 0, c == DC - 1)
                elif kind == "CB":
                    pe.wait_ge(comb_ready, k + 1)
                    settle(pe, "pe")
                    for t in range(NT):
                        ins = pe.transpose(o[0:64, t * P:(t + 1) * P], cs[:, t].bitcast(F32), ident[:])
                elif kind == "MB":
                    pe.wait_ge(combt_ready, k + 1)
                    ins = mm(o[:, 0:D], cbt[:, i * P:(i + 1) * P], bex[:])
                else:
                    t, q = divmod(i, 4)
                    tok, e2 = slice(t * P, (t + 1) * P), slice(2 * q, 2 * q + 2)
                    for c in range(DC):
                        ins = mm3(o[:], act_h[:, c, tok], act_l[:, c, tok],
                                  wex_h[:, c, e2].rearrange("p e f -> p (e f)"),
                                  wex_l[:, c, e2].rearrange("p e f -> p (e f)"), c == 0, c == DC - 1)
                ins.then_inc(gen_full, 1)

            def scores(j, n):
                b, h = divmod(n, H)
                if h == 0:
                    pe.wait_ge(qk_loaded[b], 256 * (j + 1))
                pe.wait_ge(p_ready, j * NH + n + 1 - 3 + P_CREDIT)
                for qt in range(2):
                    q0 = b * S + qt * P
                    ins = mm(sc[n % 3][:, qt * S:(qt + 1) * S], qs[:, h, q0:q0 + P], ks[:, h, b * S:(b + 1) * S])
                ins.then_inc(s_ready, 1)

            def turn(j, n):
                pe.wait_ge(p_ready, j * NH + n + 1 + P_CREDIT)
                pe.wait_ge(pts_ready[n % 2], j * NH // 2 + n // 2 + 1)
                for kt in range(2):
                    for qt in range(2):
                        ins = pe.transpose(pt[n % 2][:, kt * S + qt * P:kt * S + (qt + 1) * P],
                                           prob[:, n % 2, qt, kt * P:(kt + 1) * P], ident[:])
                ins.then_inc(pt_full, 1)

            def values(j, n):
                b, h = divmod(n, H)
                g, q = divmod(n, 4)
                pe.wait_ge(pts_ready[n % 2], j * NH // 2 + n // 2 + 2)
                if q == 0:
                    pe.wait_ge(ot_used, j * NG + g + 1)
                for kt in range(2):
                    ins = mm(ov[32 * q:32 * q + 32, 0:S], val[:, 2 * b + kt, h * VW:h * VW + 32],
                             pts[:, n % 2, kt], kt == 0, kt == 1)
                ins.then_inc(pv_done, 1)

            def turn_back(j, g):
                pe.wait_ge(ovs_ready, j * NG + g + 1)
                for qt in range(2):
                    ins = pe.transpose(ov[:, S + qt * P:S + (qt + 1) * P], ovs[:, qt * P:(qt + 1) * P], ident[:])
                ins.then_inc(ot_ready, 1)

            def slots(k, j):
                for n in range(NSLOT):
                    if n < NH:
                        scores(j, n)
                    if k is not None:
                        for u in FFN_UNITS + MID_UNITS:
                            if SLOT[u] == n:
                                unit(k, u)
                    if n >= 6 and (n - 3) % 4 == 3:
                        turn_back(j, (n - 3) // 4)
                    if 1 <= n <= NH:
                        turn(j, n - 1)
                    if 2 <= n <= NH + 1:
                        values(j, n - 2)

            for u in UNITS:
                unit(0, u)
            with pe.Fori(1, STEPS) as k:
                slots(k, k - 1)
                for u in END_UNITS:
                    unit(k, u)
            slots(None, STEPS - 1)

        @block.scalar
        def _(act):
            def hi(dst, src):
                nc.scalar.activation(dst, src, ACT.Copy).then_inc(hi_ready, 1)

            act.wait_ge(rest_loaded, 64)
            hi(wqk_h[:], wqkv_n[:, :, 0:2 * D])
            hi(wvg_h[:, :, 0:D], wqkv_n[:, :, 2 * D:3 * D])
            hi(wvg_h[:, :, D:D + E], wg_n[:])
            hi(wex_h[:], wex_n[:])
            for c in range(DC):
                for half in range(2):
                    act.wait_ge(setup_pe, 12 + 2 * c + half + 1)
                    hi(wfc_h[:, c, half * 512:(half + 1) * 512], banks[(12 + 2 * c + half) % 8][:])
            for f2 in range(FC // 2):
                act.wait_ge(setup_pe, 16 + f2 + 1)
                hi(wpj_h[:, 2 * f2:2 * f2 + 2], banks[(16 + f2) % 8][:].rearrange("p (f o) -> p f o", f=2))
            act.sem_inc(p_ready, P_CREDIT)

            def unit(k, u):
                kind, i = u
                if kind in ("CT", "XT", "ZT"):
                    full(act, k, u)
                    nc.scalar.activation(act_h[:, i], psum(u)[:], ACT.Copy).then_inc(ah_ready, 1)
                elif kind == "FC":
                    full(act, k, u)
                    wait(act, h_ready, k * FC + i - 1)
                    signal(nc.scalar.activation(gel[:, i % 2], psum(u)[:], ACT.Gelu, bias=bias_cols[:, i:i + 1]), u)
                elif kind == "A1":
                    full(act, k, u)
                    act.wait_ge(lang_loaded, 16 * 18 * (k + 1))
                    for b in range(BT):
                        tok = slice(b * S, (b + 1) * S)
                        ins = nc.scalar.activation(r1[:, tok], psum(u)[:, tok], ACT.Relu, bias=b1c[:, b:b + 1])
                    signal(ins, u)
                elif kind == "QK":
                    full(act, k, u)
                    wait(act, parts_ready, 4 * k + i - 1)
                    signal(nc.scalar.activation(qf[:, i % 2], psum(u)[:], ACT.Identity, bias=bias_cols[:, 8 + i:9 + i],
                                                scale=0.25 if i < 2 else 1.0), u)
                elif u == ("V", NT - 1):
                    act.wait_ge(lg_ready, k + 1)
                    nc.scalar.activation(ge[:], lg[:], ACT.Exp).then_inc(ge_ready, 1)
                elif kind == "CB":
                    full(act, k, u)
                    signal(nc.scalar.activation(cbt[:], psum(u)[0:64, :], ACT.Copy), u)

            def exps(j, n):
                act.wait_ge(nm_ready, j * NH + n + 1)
                act.wait_ge(pt_full, j * NH + n - 1 + PT_CREDIT)
                for qt in range(2):
                    ins = nc.scalar.activation(prob[:, n % 2, qt], sc[n % 3][:, qt * S:(qt + 1) * S], ACT.Exp,
                                               bias=nm[:, n % 4, qt:qt + 1])
                ins.then_inc(p_ready, 1)

            def slots(k, j):
                for n in range(NSLOT):
                    if n < NH:
                        exps(j, n)
                    if k is not None:
                        for u in FFN_UNITS + MID_UNITS:
                            if SLOT[u] == n:
                                unit(k, u)

            act.wait_ge(wts_ready, 1)
            for u in UNITS:
                unit(0, u)
            with act.Fori(1, STEPS) as k:
                slots(k, k - 1)
                for u in END_UNITS:
                    unit(k, u)
            slots(None, STEPS - 1)

        @block.vector
        def _(dve):
            n0 = [0]

            def link0(ins):
                n0[0] += 1
                ins.then_inc(v_step, 1)
                dve.wait_ge(v_step, n0[0])

            for half in range(2):
                dve.wait_ge(setup_pe, half + 1)
                nc.vector.tensor_copy(bt_fc[:, half * 512:(half + 1) * 512], banks[half][0:R, :]).then_inc(setup_ev, 1)
            dve.wait_ge(setup_pe, 3)
            nc.vector.tensor_copy(bt_pj[:], banks[2][0:R, 0:D]).then_inc(setup_ev, 1)
            dve.wait_ge(setup_pe, 4)
            nc.vector.tensor_copy(bias_cols[:], banks[3][:, 0:12]).then_inc(setup_ev, 1)
            dve.wait_ge(setup_ev, 4)
            link0(nc.vector.tensor_scalar(bias_cols[:, 8:10], bias_cols[:, 8:10], 0.25, None, ALU.mult))
            dve.wait_ge(w_loaded, 32)
            for i, w in enumerate((wfc_n, wpj_n)):
                nc.vector.tensor_reduce(amax[:, i:i + 1], w[:].rearrange("p c d -> p (c d)"), AX.X, ALU.max,
                                        apply_absolute_value=True).then_inc(amax_part, 1)

            def quantized(i, w, low_rank):
                dve.wait_ge(amax_all, i + 1)
                m = amax[:, 2 + i:3 + i]
                link0(nc.vector.tensor_scalar(m, m, 1.0 / QMAX, None, ALU.mult))
                link0(nc.vector.reciprocal(amax[:, i:i + 1], m))
                wf = w[:].rearrange("p c d -> p (c d)")
                q, dif = (tq1, tq2) if i == 0 else (tq1, w[:].rearrange("p c d -> p (c d)"))
                link0(nc.vector.tensor_scalar(q[:], wf, amax[:, i:i + 1], MAGIC, ALU.mult, ALU.add))
                link0(nc.vector.tensor_scalar(q[:], q[:], MAGIC, QMIN, ALU.subtract, ALU.max))
                link0(nc.vector.tensor_scalar(q[:], q[:], QMAX, m, ALU.min, ALU.mult))
                link0(nc.vector.tensor_tensor(q[:], q[:], wf, ALU.subtract))
                link0(nc.vector.tensor_tensor(q[:], q[:], wf, ALU.add))
                for jb in range(4):
                    b = 4 + 4 * i + jb
                    dve.wait_ge(setup_pe, b + 1)
                    dst = (tq2 if i == 0 else tq1)
                    ins = nc.vector.scalar_tensor_tensor(dst[:, jb * 512:(jb + 1) * 512], banks[b % 8][:], 2.0,
                                                         tq1[:, jb * 512:(jb + 1) * 512], ALU.mult, ALU.add)
                    ins.then_inc(setup_ev, 1)
                dve.wait_ge(setup_ev, 4 + 4 * i + 4)

            quantized(0, wfc_n, 0)
            dve.sem_inc(eff_ready, 1)
            quantized(1, wpj_n, 1)
            dve.sem_inc(eff_ready, 1)
            dve.wait_ge(hi_ready, 3)
            nc.vector.tensor_tensor(wqk_l[:], wqkv_n[:, :, 0:2 * D], wqk_h[:].bitcast(F32), ALU.subtract)
            nc.vector.tensor_tensor(wvg_l[:, :, 0:D], wqkv_n[:, :, 2 * D:3 * D], wvg_h[:, :, 0:D].bitcast(F32), ALU.subtract)
            nc.vector.tensor_tensor(wvg_l[:, :, D:D + E], wg_n[:], wvg_h[:, :, D:D + E].bitcast(F32), ALU.subtract)
            for jb in range(8):
                dve.wait_ge(hi_ready, 4 + jb + 1)
                o = banks[(12 + jb) % 8]
                if jb < 4:
                    c, half = divmod(jb, 2)
                    w = slice(half * 512, (half + 1) * 512)
                    ins = nc.vector.tensor_tensor(wfc_l[:, c, w], o[:], wfc_h[:, c, w].bitcast(F32), ALU.subtract)
                else:
                    f = 2 * (jb - 4)
                    ins = nc.vector.tensor_tensor(wpj_l[:, f:f + 2], o[:].rearrange("p (f o) -> p f o", f=2),
                                                  wpj_h[:, f:f + 2].bitcast(F32), ALU.subtract)
                ins.then_inc(setup_ev, 1)
            nc.vector.tensor_tensor(wex_l[:], wex_n[:], wex_h[:].bitcast(F32), ALU.subtract)
            dve.wait_ge(bex_loaded, 64)
            link0(nc.vector.tensor_copy(bex[:], bex_raw[:]))
            nc.vector.tensor_tensor(bex[32:64], bex_raw[32:64], bex[32:64].bitcast(F32), ALU.subtract)\
                .then_inc(wts_ready, 1)
            dve.wait_ge(wts_ready, 1)
            dve.wait_ge(consts_made, 1)
            for i in range(2):
                dve.sem_inc(pts_ready[i], 1)
            dve.sem_inc(ot_used, 1)

            M_STEP = 78
            m = [0]

            def link(k, ins):
                m[0] += 1
                ins.then_inc(main_step, 1)
                dve.wait_ge(main_step, k * M_STEP + m[0])

            def unit(k, u):
                kind, i = u
                o = psum(u)
                if kind in ("CT", "XT", "ZT"):
                    dve.wait_ge(ah_ready, DONE[u][1] * k + DONE[u][2] + 1)
                    signal(nc.vector.tensor_tensor(act_l[:, i], o[:], act_h[:, i].bitcast(F32), ALU.subtract), u)
                elif kind == "FC":
                    dve.wait_ge(g_ready, k * FC + i + 1)
                    link(k, nc.vector.tensor_copy(hid_h[:, i], gel[:, i % 2]))
                    nc.vector.tensor_tensor(hid_l[:, i], gel[:, i % 2], hid_h[:, i].bitcast(F32), ALU.subtract)\
                        .then_inc(h_ready, 1)
                elif kind == "PJ":
                    full(dve, k, u)
                    dve.wait_ge(xb_ready, k + 1)
                    signal(nc.vector.tensor_tensor(x1[:, i], o[:, 0:D], x[:, i, 1:D + 1], ALU.add), u)
                elif kind == "A1":
                    dve.wait_ge(r1_ready, k + 1)
                    link(k, nc.vector.tensor_copy(rs[:], r1[:]))
                    nc.vector.tensor_tensor(rs[A:P], r1[A:P], rs[A:P].bitcast(F32), ALU.subtract).then_inc(rs_ready, 1)
                elif kind == "A2":
                    full(dve, k, u)
                    dve.wait_ge(xb2_ready, k * NT + i + 1)
                    signal(nc.vector.tensor_tensor(y[:, i], o[:, 0:D], xb2[:, i], ALU.add), u)
                    dve.wait_ge(y_ready, k * NT + i + 1)
                    link(k, nc.vector.bn_stats(st[:, i], y[:, i]))
                    settle(dve, "dve")
                    link(k, nc.vector.bn_aggr(mv[:, i], st[:, i]))
                elif kind == "V":
                    full(dve, k, u)
                    nc.vector.tensor_tensor(val[:, i, 0:H * VW].rearrange("p (h w) -> p h w", w=VW)[:, :, 0:HD],
                                            o[:, 0:D].rearrange("p (h d) -> p h d", d=HD),
                                            bvg_bc[:, 0:D].rearrange("p (h d) -> p h d", d=HD), ALU.add)
                    signal(nc.vector.tensor_tensor(lg[:, i], o[:, D:D + E], bvg_bc[:, D:D + E], ALU.add), u)
                    if i == NT - 1:
                        gate_shift(k)
                elif kind == "QK":
                    dve.wait_ge(qf_ready, 4 * k + i + 1)
                    q = qf[:, i % 2]
                    link(k, nc.vector.tensor_copy(qk_parts[:, 0, i], q))
                    link(k, nc.vector.tensor_tensor(q, q, qk_parts[:, 0, i], ALU.subtract))
                    link(k, nc.vector.tensor_copy(qk_parts[:, 1, i], q))
                    nc.vector.tensor_tensor(qk_parts[:, 2, i], q, qk_parts[:, 1, i], ALU.subtract)\
                        .then_inc(parts_ready, 1)
                    if i == 0:
                        gate_top2(k)
                elif kind == "MB":
                    full(dve, k, u)
                    if i == 0:
                        wait(dve, stored, 16 * BT * k)
                    signal(nc.vector.tensor_tensor(acc[:, i], o[:, 0:D], x1[:, i], ALU.add), u)
                elif kind == "ME":
                    full(dve, k, u)
                    t, q = divmod(i, 4)
                    dve.wait_ge(moe_added, DONE[u][1] * k + DONE[u][2])
                    link(k, nc.vector.scalar_tensor_tensor(acc[:, t], o[:, 0:D], cmb[:, t, 2 * q:2 * q + 1], acc[:, t],
                                                           ALU.mult, ALU.add))
                    signal(nc.vector.scalar_tensor_tensor(acc[:, t], o[:, D:2 * D], cmb[:, t, 2 * q + 1:2 * q + 2],
                                                          acc[:, t], ALU.mult, ALU.add), u)

            def wide(v):
                return v.unsqueeze(2).to_broadcast([P, NT, E])

            def gate_shift(k):
                dve.wait_ge(v_ready, (k + 1) * NT)
                link(k, nc.vector.tensor_reduce(gm[:], lg[:], AX.X, ALU.max))
                nc.vector.tensor_tensor(lg[:], lg[:], wide(gm[:]), ALU.subtract).then_inc(lg_ready, 1)

            def gate_top2(k):
                dve.wait_ge(ge_ready, k + 1)
                link(k, nc.vector.tensor_reduce(gm[:], ge[:], AX.X, ALU.add))
                link(k, nc.vector.reciprocal(gm[:], gm[:]))
                link(k, nc.vector.tensor_tensor(gt[:], ge[:], wide(gm[:]), ALU.mult))
                for g, s in ((gt, s1), (g2, s2)):
                    link(k, nc.vector.tensor_reduce(gm[:], g[:], AX.X, ALU.max))
                    link(k, nc.vector.tensor_tensor(eq[:], g[:], wide(gm[:]), ALU.is_equal))
                    link(k, nc.vector.tensor_tensor(eq[:], eq[:], rank_row[:].unsqueeze(1).to_broadcast([P, NT, E]),
                                                    ALU.mult))
                    link(k, nc.vector.tensor_reduce(gm[:], eq[:], AX.X, ALU.max))
                    link(k, nc.vector.tensor_tensor(s[:], eq[:], wide(gm[:]), ALU.is_equal))
                    if g is gt:
                        link(k, nc.vector.scalar_tensor_tensor(g2[:], s1[:], -2.0, gt[:], ALU.mult, ALU.add))
                link(k, nc.vector.tensor_tensor(s1[:], s1[:], s2[:], ALU.add))
                link(k, nc.vector.tensor_tensor(cmb[:], s1[:], gt[:], ALU.mult))
                nc.vector.tensor_copy(cs[:, :, 0:E], cmb[:])
                link(k, nc.vector.tensor_copy(cs[:, :, 32:32 + E], cmb[:]))
                nc.vector.tensor_tensor(cs[:, :, E:2 * E], cmb[:], cs[:, :, 0:E].bitcast(F32), ALU.subtract)
                nc.vector.tensor_tensor(cs[:, :, 32 + E:32 + 2 * E], cmb[:], cs[:, :, 0:E].bitcast(F32), ALU.subtract)\
                    .then_inc(comb_ready, 1)

            def split_languages(k):
                dve.wait_ge(lang_loaded, 16 * 18 * (k + 1))
                w1 = wraw[:, 0].rearrange("p b (c m) -> p b c m", c=DC)
                nc.vector.tensor_copy(w1_h[:], w1)
                link(k, nc.vector.tensor_copy(w2_h[:], wraw[:, 1]))
                nc.vector.tensor_tensor(w1_l[:], w1, w1_h[:].bitcast(F32), ALU.subtract)
                nc.vector.tensor_tensor(w2_l[:], wraw[:, 1], w2_h[:].bitcast(F32), ALU.subtract).then_inc(lang_split, 1)

            def normalize(k):
                link(k, nc.vector.tensor_scalar(ve[:], mv[:, :, 1], LN_EPS, None, ALU.add))
                link(k, nc.vector.tensor_scalar(rsd[:].bitcast(I32), ve[:].bitcast(I32), -0.5, RSQRT_SEED,
                                                ALU.mult, ALU.add))
                for _ in range(4):
                    link(k, nc.vector.scalar_tensor_tensor(rst[:], rsd[:], -0.5, rsd[:], ALU.mult, ALU.mult))
                    link(k, nc.vector.tensor_tensor(rst[:], rst[:], ve[:], ALU.mult))
                    link(k, nc.vector.scalar_tensor_tensor(rsd[:], rst[:], 1.5, rsd[:], ALU.add, ALU.mult))
                for t in range(NT):
                    nc.vector.tensor_scalar(y[:, t], y[:, t], mv[:, t, 0:1], rsd[:, t:t + 1], ALU.subtract, ALU.mult)\
                        .then_inc(zn_ready, 1)

            def main_units(k, us):
                for u in us:
                    unit(k, u)
                    if u == ("FC", FC - 1):
                        split_languages(k)
                    if u == ("A2", NT - 1):
                        normalize(k)

            A_STEP = NG
            s = [0]

            def alink(j, ins):
                s[0] += 1
                ins.then_inc(att_step, 1)
                dve.wait_ge(att_step, j * A_STEP + s[0])

            def slots(k, j):
                s[0] = 0
                for n in range(NSLOT):
                    g = (n - 3) // 4
                    back = n >= 6 and (n - 3) % 4 == 3
                    if back:
                        dve.wait_ge(pv_done, j * NH + 4 * g + 4 + PV_CREDIT)
                        nc.vector.tensor_copy(ovs[:], ov[:, 0:S]).then_inc(ovs_ready, 1)
                    if n < NH:
                        dve.wait_ge(s_ready, j * NH + n + 1)
                        nc.vector.tensor_reduce(nm[:, n % 4], sc[n % 3][:].rearrange("p (q k) -> p q k", q=2), AX.X,
                                                ALU.max, negate=True).then_inc(nm_ready, 1)
                    if k is not None:
                        main_units(k, [u for u in FFN_UNITS + MID_UNITS if SLOT[u] == n])
                    if back:
                        b, gb = divmod(g, NG // BT)
                        dve.wait_ge(ot_ready, j * NG + g + 1)
                        o = ov[:, S:2 * S].rearrange("p (q h w) -> p q h w", q=2, h=4)
                        alink(j, nc.vector.reciprocal(rden[:], o[:, :, :, HD:VW]))
                        nc.vector.tensor_tensor(tmp[:], o[:, :, :, 0:HD], rden[:].to_broadcast([P, 2, 4, HD]),
                                                ALU.mult).then_inc(ot_used, 1)
                        dve.wait_ge(ot_used, j * NG + g + 2)
                        dst = acc[:, 2 * b:2 * b + 2, gb * 4 * HD:(gb + 1) * 4 * HD]
                        nc.vector.tensor_tensor(dst, dst, tmp[:].rearrange("p q h w -> p q (h w)"), ALU.add)\
                            .then_inc(att_added, 1)
                    if 1 <= n <= NH:
                        i = n - 1
                        dve.wait_ge(pt_full, j * NH + i + 1 + PT_CREDIT)
                        dve.wait_ge(pv_done, j * NH + i - 1 + PV_CREDIT)
                        nc.vector.tensor_copy(pts[:, i % 2].rearrange("p a b -> p (a b)"), pt[i % 2][:])\
                            .then_inc(pts_ready[i % 2], 1)

            def done():
                assert m[0] == M_STEP, m[0]
                m[0] = 0

            main_units(0, UNITS)
            done()
            with dve.Fori(1, STEPS) as k:
                slots(k, k - 1)
                main_units(k, END_UNITS)
                done()
            slots(None, STEPS - 1)


_INS = ["x", "condB_zX", "condB_zY", "condB_zR", "itok_B_0_8", "L0_ffn_W_fc", "L0_ffn_b_fc", "L0_ffn_A_fc",
        "L0_ffn_B_fc", "L0_ffn_W_proj", "L0_ffn_b_proj", "L0_ffn_A_proj", "L0_ffn_B_proj", "L1_cond_W1",
        "L1_cond_b1", "L1_cond_W2", "L1_cond_b2", "L1_cond_gamma", "L1_cond_beta", "L1_ffn_W_qkv",
        "L1_ffn_b_qkv", "L1_ffn_W_gate", "L1_ffn_b_gate", "L1_ffn_W_experts", "L1_ffn_b_experts"]


def kernel(**inputs):
    import numpy as np
    import concourse.bacc as bacc
    from concourse.bass_utils import run_bass_kernel_spmd

    nc = bacc.Bacc("TRN2", target_bir_lowering=False, num_devices=1)
    arrays, aps = {}, {}
    for name in _INS:
        v = np.ascontiguousarray(inputs[name])
        arrays[f"in_{name}"] = v
        aps[name] = nc.dram_tensor(f"in_{name}", v.shape, mybir.dt.from_np(v.dtype), kind="ExternalInput").ap()
    out = nc.dram_tensor("out", (B, S, D), F32, kind="ExternalOutput").ap()
    block_kernel(nc, aps, out)
    return run_bass_kernel_spmd(nc, [arrays], core_ids=[0]).results[0]["out"]
```

```python
from contextlib import ExitStack

import concourse.bass as bass
from concourse import mybir

ALU = mybir.AluOpType
ACT = mybir.ActivationFunctionType
AX = mybir.AxisListType
F32 = mybir.dt.float32
F32R = mybir.dt.float32r
BF16 = mybir.dt.bfloat16
I32 = mybir.dt.int32

P = 128
B, S, D = 16, 256, 256
F = 1024
H, HD = 16, 16
E = 8
A = 64
R = 16
L = 10

BT = 2
TOK = BT * S
STEPS = B // BT
NT = TOK // P
DC = D // P
FC = F // P
NH = BT * H
NG = NH // 4
VW = HD + 1
QMAX, QMIN = 127.0, -128.0
MAGIC = 1.5 * 2.0**23
LN_EPS = 1e-5
RSQRT_SEED = 1597463007.0

Q_PART = (0, 0, 1, 1, 0, 2, 1, 2)
K_PART = (0, 1, 0, 1, 2, 0, 2, 1)

NEWTON = 3
FREE_WORK = [("W", 0), ("ST", 0), ("ST", 1), ("SPLIT", 0)] + [("LN", i) for i in range(NEWTON + 2)] + [("GATE", i) for i in range(4)]
SLOTTED = (
    [("W", 0), ("ST", 0), ("ST", 1)]
    + [("CT", c) for c in range(DC)]
    + [("FC", f) for f in range(FC)]
    + [("PJ", 0), ("PJ", 1), ("SPLIT", 0), ("PJ", 2), ("PJ", 3)]
    + [("XT", c) for c in range(DC)]
    + [("A1", 0)]
    + [("A2", t) for t in range(NT)]
    + [("LN", i) for i in range(NEWTON + 2)]
    + [("ZT", c) for c in range(DC)]
    + [("LG", 0)]
    + [("QK", 0), ("LT", 0), ("GATE", 0), ("QK", 1), ("GATE", 1), ("QK", 2), ("GATE", 2), ("QK", 3), ("GATE", 3)]
    + [("V", t) for t in range(NT)]
)
EXPERTS = [("ME", 4 * t + q) for q in range(4) for t in range(NT // BT)]
EXPERTS = EXPERTS[:1] + [("CB", 0)] + EXPERTS[1:] + [("MB", t) for t in range(NT)]
LATE_EXPERTS = [("ME", 4 * t + q) for q in range(4) for t in range(NT // BT, NT)]
ADDS = [u for u in EXPERTS + LATE_EXPERTS if u != ("CB", 0)]
UNITS = [u for u in SLOTTED + EXPERTS + LATE_EXPERTS if u not in FREE_WORK]
NU = len(UNITS)
SHADE = {'W': [2], 'ST': [5, 6], 'CT': [7, 7], 'FC': [9, 9, 9, 9, 9, 9, 9, 9], 'PJ': [11, 12, 13, 13], 'SPLIT': [12], 'XT': [14, 14], 'A1': [16], 'A2': [18, 18, 18, 18], 'LN': [18, 18, 20, 21, 22], 'ZT': [23, 23], 'LG': [24], 'QK': [25, 28, 30, 32], 'LT': [25], 'GATE': [26, 28, 30, 32], 'V': [34, 35, 35, 37]}
LATE_SLOTS = (0, 0, 1, 1, 2, 2, 3, 4)
LAG_ACT, LAG_DVE = {'PJ': 1, 'A2': 1}, {'XT': 1, 'QK': 1, 'ZT': 1, 'CT': 1}
SLOT = {(kind, i): n for kind, at in SHADE.items() for i, n in enumerate(at)}
SLOT |= {u: n for u, n in zip(LATE_EXPERTS, LATE_SLOTS)}
TURN_BACK, NORM = 8, 9
NSLOT = NH - 4 + NORM + 1
BANK = {}
for _i, _u in enumerate(u for u in UNITS if u in SLOTTED):
    BANK[_u] = 6 + _i % 2
for _i, _u in enumerate(EXPERTS):
    BANK[_u] = (7, 0, 1, 6)[_i % 4]
for _i, _u in enumerate(LATE_EXPERTS):
    BANK[_u] = 6 + _i % 2


def before(u):
    at = UNITS.index(u)
    for i in range(at - 1, at - NU - 1, -1):
        if BANK[UNITS[i]] == BANK[u]:
            return UNITS[i], i < 0


def shade(k, j, n, lag={}):
    for u in LATE_EXPERTS + (SLOTTED if k is not None else []):
        if SLOT[u] + lag.get(u[0], 0) == n:
            yield (j if u in LATE_EXPERTS else k), u


def wait(eng, sem, value):
    if isinstance(value, int) and value <= 0:
        return
    eng.wait_ge(sem, value)


def block_kernel(nc, a, out):
    scr = nc.dram_tensor("qk_parts", (2, 3, D, TOK), BF16, kind="Internal").ap()
    ctx = ExitStack()
    with ctx:
        top = [(nc.sbuf_base + 63) // 64 * 64]

        def sb(name, shape, dt=F32, at=None):
            n = 1
            for s in shape[1:]:
                n *= s
            n = (n * (2 if dt == BF16 else 4) + 63) // 64 * 64
            if at is None:
                at = top[0]
                top[0] += n
            t = nc.alloc_sbuf_tensor_at(name, shape, dt, offset=at)
            return t

        def region(nbytes):
            at = top[0]
            top[0] += nbytes
            return at

        def sem(name):
            return ctx.enter_context(nc.semaphore(name))

        ident = sb("ident", [P, P])
        wfc_h, wfc_l = sb("wfc_h", [P, DC, F], F32R), sb("wfc_l", [P, DC, F], F32R)
        wpj_h, wpj_l = sb("wpj_h", [P, FC, D], F32R), sb("wpj_l", [P, FC, D], F32R)
        wqk_h, wqk_l = sb("wqk_h", [P, DC, 2 * D], F32R), sb("wqk_l", [P, DC, 2 * D], F32R)
        wv_h, wv_l = sb("wv_h", [P, DC, D], F32R), sb("wv_l", [P, DC, D], F32R)
        wg_h, wg_l = sb("wg_h", [P, DC, E], F32R), sb("wg_l", [P, DC, E], F32R)
        wex_h, wex_l = sb("wex_h", [P, DC, E, D], F32R), sb("wex_l", [P, DC, E, D], F32R)
        bex = sb("bex", [64, D], F32R)
        bias_cols = sb("bias_cols", [P, 12])
        bpj_bc = sb("bpj_bc", [P, D])
        bv_bc, bg_col = sb("bv_bc", [P, D]), sb("bg_col", [E, 1])
        rank_row = sb("rank_row", [P, E])
        z_all = sb("z_all", [P, 4, B])
        z_cur = sb("z_cur", [P, 4, BT])

        h_at = region(2 * FC * TOK * 4)
        hid_h = sb("hid_h", [P, FC, TOK], F32R, at=h_at)
        hid_l = sb("hid_l", [P, FC, TOK], F32R, at=h_at + FC * TOK * 4)
        qk_parts = sb("qk_parts_sb", [P, 3, 4, TOK], BF16, at=h_at)
        qk_at = region(2 * H * TOK * 2)
        qs = sb("qs", [P, H, TOK], BF16, at=qk_at)
        ks = sb("ks", [P, H, TOK], BF16, at=qk_at + H * TOK * 2)
        act_h, act_l = sb("act_h", [P, DC, TOK], F32R), sb("act_l", [P, DC, TOK], F32R)
        x = sb("x", [P, NT, D + 2])
        u_at, d_at, t_at = region(4096), region(4096), region(4096)
        up = sb("up", [P, NT, D], at=u_at)
        wraw = sb("wraw", [P, 2, BT, D], at=u_at)
        y = sb("y", [P, NT, D], at=u_at)
        dn = sb("dn", [P, NT, D], at=d_at)
        xb2 = sb("xb2", [P, NT, D], at=d_at)
        lap = sb("lap", [P, NT, D], at=t_at)
        gel = sb("gel", [P, 2, TOK], at=t_at)
        qf = sb("qf", [P, 2, TOK], at=t_at)
        r1 = sb("r1", [P, TOK], at=t_at)
        rs = sb("rs", [P, TOK], F32R, at=t_at + TOK * 4)
        lgt = sb("lgt", [E, TOK], at=t_at + TOK * 4)
        x1 = sb("x1", [P, NT, D])
        acc = sb("acc", [P, NT, D])
        val = sb("val", [P, NT, H * VW + 16])
        p_at, pts_at = region(4096), region(4096)
        prob = sb("prob", [P, 2, 2, S], at=p_at)
        pts = sb("pts", [P, 2, 2, S], at=pts_at)
        ovs = sb("ovs", [P, S])
        tmp = sb("tmp", [P, 2, 4, HD])
        rden = sb("rden", [P, 2, 4, 1])
        nm = sb("nm", [P, 4, 2])
        bc = sb("bc", [P, BT, 3, D])
        w1_h, w1_l = sb("w1_h", [P, BT, DC, P], F32R), sb("w1_l", [P, BT, DC, P], F32R)
        w2_h, w2_l = sb("w2_h", [P, BT, D], F32R), sb("w2_l", [P, BT, D], F32R)
        b1c = sb("b1c", [P, BT])
        st = sb("st", [P, NT, 6])
        mv = sb("mv", [P, NT, 2])
        ve, rsd, rst = sb("ve", [P, NT]), sb("rsd", [P, NT]), sb("rst", [P, NT])
        lg, ge, gt, g2 = (sb(n, [P, NT, E]) for n in ("lg", "ge", "gt", "g2"))
        eq, s1, s2, cmb = (sb(n, [P, NT, E]) for n in ("eq", "s1", "s2", "cmb"))
        gm = sb("gm", [P, NT])
        cs = sb("cs", [P, NT, 64], F32R)
        cbt = sb("cbt", [64, TOK], F32R, at=pts_at)
        amax = sb("amax", [P, 4])
        assert top[0] <= nc.sbuf_base + 212863, top[0]

        wfc_n = sb("wfc_n", [P, FC, D], at=h_at)
        wpj_n = sb("wpj_n", [P, DC, F], at=h_at + 8192)
        tq1 = sb("tq1", [P, 2048], at=h_at + 16384)
        tq2 = sb("tq2", [P, 2048], at=h_at + 24576)
        wex_n = sb("wex_n", [P, DC, E, D], at=qk_at)
        wqkv_n = sb("wqkv_n", [P, DC, 3 * D], at=qk_at + 16384)
        wg_n = sb("wg_n", [P, DC, E], at=qk_at + 22528)
        a_fc = sb("a_fc", [R, D], at=qk_at + 22592)
        b_fcn = sb("b_fcn", [P, FC, R], at=qk_at + 23616)
        b_pjn = sb("b_pjn", [P, DC, R], at=qk_at + 24128)
        bt_pj = sb("bt_pj", [R, D], at=qk_at + 24256)
        bias_rows = sb("bias_rows", [12, P], at=qk_at + 25600)
        bex_raw = sb("bex_raw", [64, D], at=qk_at + 26112)
        bt_fc = sb("bt_fc", [R, F], at=p_at)
        a_pj = sb("a_pj", [R, F], at=pts_at)

        banks = [ctx.enter_context(nc.psum_tensor(f"bank{i}", [P, 512], F32)) for i in range(8)]
        sc = banks[0:2]
        pt = banks[2:4]
        ov = banks[4:6]

        w_loaded = [sem(f"w_loaded{i}") for i in range(2)]
        z_loaded = sem("z_loaded")
        factors_ready = sem("factors_ready")
        lo_ready = sem("lo_ready")
        wex_ready = sem("wex_ready")
        z_made = sem("z_made")
        lora_loaded = sem("lora_loaded")
        rest_loaded = sem("rest_loaded")
        bias_loaded = sem("bias_loaded")
        bex_loaded = sem("bex_loaded")
        bex_zeroed = sem("bex_zeroed")
        ident_made = sem("ident_made")
        consts_made = sem("consts_made")
        amax_part = sem("amax_part")
        amax_all = sem("amax_all")
        setup_pe = sem("setup_pe")
        eff_ready = sem("eff_ready")
        hi_ready = sem("hi_ready")
        v_step = sem("v_step")
        p_step = sem("p_step")

        first_x_loaded = sem("first_x_loaded")
        x_loaded = sem("x_loaded")
        c_ready = sem("c_ready")
        xb_ready = sem("xb_ready")
        sums_ready = sem("sums_ready")
        w_ready = sem("w_ready")
        wx_ready = sem("wx_ready")
        ah_ready = sem("ah_ready")
        at_ready = sem("at_ready")
        g_ready = sem("g_ready")
        h_ready = sem("h_ready")
        x1_ready = sem("x1_ready")
        xb2_ready = sem("xb2_ready")
        lang_loaded = sem("lang_loaded")
        lang_split = sem("lang_split")
        r1_ready = sem("r1_ready")
        rs_ready = sem("rs_ready")
        y_ready = sem("y_ready")
        st_ready = sem("st_ready")
        mv_ready = sem("mv_ready")
        centered = sem("centered")
        z_ready = sem("z_ready")
        v_ready = sem("v_ready")
        qf_ready = sem("qf_ready")
        parts_ready = sem("parts_ready")
        scr_written = sem("scr_written")
        qk_loaded = [sem(f"qk_loaded{b}") for b in range(BT)]
        lgt_ready = sem("lgt_ready")
        logits_made = sem("logits_made")
        lg_ready = sem("lg_ready")
        ge_ready = sem("ge_ready")
        comb_ready = sem("comb_ready")
        combt_ready = sem("combt_ready")
        moe_added = sem("moe_added")
        gen_full = sem("gen_full")
        main_step = sem("main_step")
        att_step = sem("att_step")

        s_ready = sem("s_ready")
        nm_ready = sem("nm_ready")
        p_ready = sem("p_ready")
        pt_full = sem("pt_full")
        pts_ready = sem("pts_ready")
        pv_done = sem("pv_done")
        ovs_ready = sem("ovs_ready")
        ot_ready = sem("ot_ready")
        ot_used = sem("ot_used")
        att_added = sem("att_added")
        stored = [sem(f"stored{b}") for b in range(BT)]

        settled = {n: sem(f"settled_{n}") for n in ("sp", "pool", "pe", "dve")}

        def settle(eng, name):
            eng.sem_inc(settled[name], 1)

        WEIGHTS_FOR = {("CT", 0): 4, ("PJ", 0): 8, ("LG", 0): 11, ("MB", 0): 12}

        DONE = {}
        for c in range(DC):
            DONE[("CT", c)] = (at_ready, 3 * DC, c)
            DONE[("XT", c)] = (at_ready, 3 * DC, DC + c)
            DONE[("ZT", c)] = (at_ready, 3 * DC, 2 * DC + c)
        for f in range(FC):
            DONE[("FC", f)] = (g_ready, FC, f)
        for t in range(NT):
            DONE[("PJ", t)] = (x1_ready, NT, t)
            DONE[("A2", t)] = (y_ready, NT, t)
            DONE[("V", t)] = (v_ready, NT, t)
            DONE[("QK", t)] = (qf_ready, 4, t)
        DONE[("A1", 0)] = (r1_ready, 1, 0)
        for i, u in enumerate(ADDS):
            DONE[u] = (moe_added, len(ADDS), i)
        DONE[("LG", 0)] = (lgt_ready, 1, 0)
        DONE[("LT", 0)] = (logits_made, 1, 0)
        DONE[("CB", 0)] = (combt_ready, 1, 0)

        def full(eng, k, unit):
            eng.wait_ge(gen_full, k * NU + UNITS.index(unit) + 1)

        def signal(ins, unit):
            ins.then_inc(DONE[unit][0], 1)

        def psum(unit):
            return banks[BANK[unit]]

        P_CREDIT, PT_CREDIT, PTS_CREDIT, PV_CREDIT, OT_CREDIT = 2, 2, 2, 2, 2

        block = ctx.enter_context(nc.Block())

        def load_x(eng, xs, loaded):
            for b in range(BT):
                eng.dma_start(x[:, 2 * b:2 * b + 2, 1:D + 1],
                              xs[b].rearrange("(t p) d -> p t d", p=P)).then_inc(loaded, 16)

        def load_rows(eng, xs, loaded):
            for b in range(BT):
                t0, t1 = 2 * b, 2 * b + 1
                eng.dma_start(up[1:P, t0], xs[b, 0:P - 1]).then_inc(loaded, 16)
                eng.dma_start(up[0:1, t0], xs[b, 1:2]).then_inc(loaded, 16)
                eng.dma_start(up[:, t1], xs[b, P - 1:2 * P - 1]).then_inc(loaded, 16)
                eng.dma_start(dn[:, t0], xs[b, 1:P + 1]).then_inc(loaded, 16)
                eng.dma_start(dn[0:P - 1, t1], xs[b, P + 1:2 * P]).then_inc(loaded, 16)
                eng.dma_start(dn[P - 1:P, t1], xs[b, 2 * P - 2:2 * P - 1]).then_inc(loaded, 16)

        @block.sync
        def _(sp):
            sp.dma_start(wfc_n[:], a["L0_ffn_W_fc"].rearrange("(c p) d -> p c d", p=P)).then_inc(w_loaded[0], 16)
            sp.dma_start(b_fcn[:], a["L0_ffn_B_fc"].rearrange("(c p) r -> p c r", p=P)).then_inc(lora_loaded, 16)
            sp.dma_start(b_pjn[:], a["L0_ffn_B_proj"].rearrange("(c p) r -> p c r", p=P)).then_inc(lora_loaded, 16)
            sp.dma_start(wpj_n[:], a["L0_ffn_W_proj"].rearrange("(c p) f -> p c f", p=P)).then_inc(w_loaded[1], 16)
            sp.dma_start(a_fc[:], a["L0_ffn_A_fc"]).then_inc(lora_loaded, 16)
            sp.dma_start(a_pj[:], a["L0_ffn_A_proj"]).then_inc(lora_loaded, 16)
            sp.dma_start(bias_rows[0:8, :], a["L0_ffn_b_fc"].rearrange("(c p) -> c p", p=P)).then_inc(lora_loaded, 16)
            sp.dma_start(bias_rows[8:12, :], a["L1_ffn_b_qkv"][0:2 * D].rearrange("(c p) -> c p", p=P)).then_inc(lora_loaded, 16)
            for i, n in enumerate(("condB_zX", "condB_zY", "condB_zR")):
                sp.dma_start(z_all[:, i, :], a[n].partition_broadcast(P)).then_inc(z_loaded, 16)
            load_x(sp, a["x"][0:BT], first_x_loaded)
            load_rows(sp, a["x"][0:BT], first_x_loaded)
            for dst, src in ((bpj_bc[:], a["L0_ffn_b_proj"]), (bv_bc[:], a["L1_ffn_b_qkv"][2 * D:3 * D])):
                sp.dma_start(dst, src.partition_broadcast(P)).then_inc(bias_loaded, 16)
            with nc.allow_non_contiguous_dma(reason="one bias for each partition"):
                sp.dma_start(bg_col[:], a["L1_ffn_b_gate"].rearrange("(e o) -> e o", o=1)).then_inc(bias_loaded, 16)
            sp.dma_start(wqkv_n[:], a["L1_ffn_W_qkv"].rearrange("(c p) n -> p c n", p=P)).then_inc(rest_loaded, 16)
            sp.dma_start(wg_n[:], a["L1_ffn_W_gate"].rearrange("(c p) n -> p c n", p=P)).then_inc(rest_loaded, 16)
            for c in range(DC):
                sp.dma_start(wex_n[:, c], a["L1_ffn_W_experts"][:, c * P:(c + 1) * P, :].rearrange("e p f -> p e f"))\
                    .then_inc(rest_loaded, 16)
            sp.wait_ge(bex_zeroed, 1)
            for r in (0, 8, 32, 40):
                sp.dma_start(bex_raw[r:r + E, :], a["L1_ffn_b_experts"]).then_inc(bex_loaded, 16)

            def languages(k):
                sp.wait_ge(at_ready, k * 3 * DC + DC)
                settle(sp, "sp")
                for b in range(BT):
                    lang = sp.value_load(a["itok_B_0_8"].rearrange("(o n) -> o n", o=1)[:, bass.ds(k * BT + b, 1)],
                                         min_val=0, max_val=L - 1)
                    w1 = a["L1_cond_W1"][bass.ds(lang, 1)].rearrange("l (c p) a -> p (l c) a", p=P)
                    w2 = a["L1_cond_W2"][bass.ds(lang, 1)].rearrange("l a h -> (l a) h")
                    b1 = a["L1_cond_b1"][bass.ds(lang, 1)].rearrange("l a -> a l")
                    for half in range(2):
                        sp.dma_start(wraw[:, 0, b].rearrange("p (c m) -> p c m", c=DC)[:, :, half * A:(half + 1) * A], w1)\
                            .then_inc(lang_loaded, 16)
                        sp.dma_start(wraw[half * A:(half + 1) * A, 1, b], w2).then_inc(lang_loaded, 16)
                        with nc.allow_non_contiguous_dma(reason="one bias for each partition"):
                            sp.dma_start(b1c[half * A:(half + 1) * A, b:b + 1], b1).then_inc(lang_loaded, 16)
                    for i, n in enumerate(("L1_cond_b2", "L1_cond_gamma", "L1_cond_beta")):
                        sp.dma_start(bc[:, b, i], a[n][bass.ds(lang, 1)].rearrange("l h -> (l h)").partition_broadcast(P))\
                            .then_inc(lang_loaded, 16)

            def store(j, b):
                sp.wait_ge(att_added, j * NG + (b + 1) * NG // BT)
                settle(sp, "sp")
                sp.dma_start(out[bass.ds(j * BT + b, 1)].rearrange("b (t p) d -> p (b t) d", p=P),
                             acc[:, 2 * b:2 * b + 2]).then_inc(stored[b], 16)

            def write_parts(k):
                for m in range(4):
                    sp.wait_ge(parts_ready, 4 * k + m + 1)
                    sp.dma_start(scr[m // 2, :, (m % 2) * P:(m % 2 + 1) * P, :].rearrange("s p t -> p s t"),
                                 qk_parts[:, :, m, :]).then_inc(scr_written, 16)

            def read_parts(k):
                sp.wait_ge(scr_written, 64 * (k + 1))
                for b in range(BT):
                    for i, (dst, part) in enumerate(((qs, Q_PART), (ks, K_PART))):
                        for c in range(8):
                            sp.dma_start(dst[16 * c:16 * c + 16, :, b * S:(b + 1) * S],
                                         scr[i, part[c], :, b * S:(b + 1) * S].rearrange("(h d) t -> d h t", d=HD))\
                                .then_inc(qk_loaded[b], 16)

            languages(0)
            write_parts(0)
            sp.wait_ge(wex_ready, 1)
            read_parts(0)
            with sp.Fori(1, STEPS) as k:
                languages(k)
                store(k - 1, 0)
                write_parts(k)
                store(k - 1, 1)
                read_parts(k)
            store(STEPS - 1, 0)
            store(STEPS - 1, 1)
            for b in range(BT):
                sp.wait_ge(stored[b], 16 * STEPS)

        @block.gpsimd
        def _(pool):
            nc.gpsimd.memset(ident[:], 0.0).then_inc(p_step, 1)
            nc.gpsimd.memset(bex_raw[:], 0.0).then_inc(bex_zeroed, 1)
            pool.wait_ge(p_step, 1)
            nc.gpsimd.affine_select(out=ident[:], in_=ident[:], compare_op=ALU.not_equal, fill=1.0, base=0,
                                    pattern=[[-1, P]], channel_multiplier=1).then_inc(ident_made, 1)
            for e in range(E):
                nc.gpsimd.memset(rank_row[:, e:e + 1], float(E - e))
            nc.gpsimd.memset(val[:], 0.0).then_inc(p_step, 1)
            pool.wait_ge(p_step, 2)
            nc.gpsimd.memset(val[:, :, 0:H * VW].rearrange("p t (h w) -> p t h w", w=VW)[:, :, :, HD:VW], 1.0)
            nc.gpsimd.memset(cs[:].bitcast(F32), 0.0).then_inc(consts_made, 1)
            for i in range(2):
                pool.wait_ge(amax_part, i + 1)
                nc.gpsimd.partition_all_reduce(amax[:, 2 + i:3 + i], amax[:, i:i + 1], P,
                                               bass.bass_isa.ReduceOp.max).then_inc(amax_all, 1)
            pool.wait_ge(z_made, 1)
            pool.wait_ge(bias_loaded, 16 * 3)

            xi = x[:, :, 1:D + 1]
            N_STEP = 1

            def main(k):
                base = 2 + k * N_STEP
                n = [0]

                def link(ins):
                    n[0] += 1
                    ins.then_inc(p_step, 1)
                    pool.wait_ge(p_step, base + n[0])
                    settle(pool, "pool")

                if not (isinstance(k, int) and k == 0):
                    xs = a["x"][bass.ds(k * BT, BT)]
                    pool.wait_ge(x1_ready, k * NT)
                    settle(pool, "pool")
                    load_x(pool, xs, x_loaded)
                    pool.wait_ge(at_ready, k * 3 * DC)
                    settle(pool, "pool")
                    load_rows(pool, xs, x_loaded)
                nc.gpsimd.tensor_copy(z_cur[:], z_all[:, :, bass.ds(k * BT, BT)])
                if isinstance(k, int) and k == 0:
                    pool.wait_ge(first_x_loaded, 16 * 14)
                else:
                    pool.wait_ge(x_loaded, 16 * 14 * k)
                settle(pool, "pool")
                nc.gpsimd.tensor_copy(x[:, :, 0:1], x[:, :, 2:3])
                link(nc.gpsimd.tensor_copy(x[:, :, D + 1:D + 2], x[:, :, D - 1:D]))
                nc.gpsimd.tensor_tensor(dn[:], up[:], dn[:], ALU.add)
                wait(pool, parts_ready, k * 4)
                nc.gpsimd.tensor_tensor(lap[:], x[:, :, 0:D], x[:, :, 2:D + 2], ALU.add).then_inc(sums_ready, 1)
                pool.wait_ge(w_ready, k + 1)
                nc.gpsimd.tensor_tensor(up[:], up[:], xi, ALU.mult).then_inc(wx_ready, 1)
                nc.gpsimd.tensor_tensor(xi, xi, bpj_bc[:].unsqueeze(1).to_broadcast([P, NT, D]), ALU.add)\
                    .then_inc(xb_ready, 1)
                pool.wait_ge(lang_loaded, 16 * 18 * (k + 1))
                for t in range(NT):
                    pool.wait_ge(x1_ready, k * NT + t + 1)
                    nc.gpsimd.tensor_tensor(xb2[:, t], x1[:, t], bc[:, t // 2, 0], ALU.add).then_inc(xb2_ready, 1)
                assert n[0] == N_STEP, n[0]

            main(0)
            pool.wait_ge(hi_ready, 12)
            nc.gpsimd.tensor_tensor(wex_l[:], wex_n[:], wex_h[:].bitcast(F32), ALU.subtract).then_inc(wex_ready, 1)
            with pool.Fori(1, STEPS) as k:
                main(k)

        @block.tensor
        def _(pe):
            def mm(o, l, r, start=True, stop=True):
                return pe.matmul(o, l, r, start=start, stop=stop)

            def mm3(o, lh, ll, rh, rl, start, stop):
                mm(o, lh, rh, start, False)
                mm(o, lh, rl, False, False)
                return mm(o, ll, rh, False, stop)

            pe.wait_ge(ident_made, 1)
            pe.wait_ge(lora_loaded, 16 * 6)
            for half in range(2):
                for i in range(4):
                    ins = pe.transpose(banks[half][0:R, i * P:(i + 1) * P], b_fcn[:, 4 * half + i], ident[:])
                ins.then_inc(setup_pe, 1)
            for c in range(DC):
                ins = pe.transpose(banks[2][0:R, c * P:(c + 1) * P], b_pjn[:, c], ident[:])
            ins.then_inc(setup_pe, 1)
            pe.transpose(banks[3][:, 0:12], bias_rows[:], ident[0:12, 0:12]).then_inc(setup_pe, 1)
            pe.wait_ge(factors_ready, 4)
            for c in range(DC):
                for half in range(2):
                    mm(banks[4 + 2 * c + half][:], a_fc[:, c * P:(c + 1) * P], bt_fc[:, half * 512:(half + 1) * 512],
                       True, False)
            pe.wait_ge(eff_ready, 1)
            for c in range(DC):
                for half in range(2):
                    for i in range(4):
                        f = 4 * half + i
                        ins = mm(banks[4 + 2 * c + half][:, i * P:(i + 1) * P],
                                 tq1[:, f * D + c * P:f * D + (c + 1) * P], ident[:], False, i == 3)
                    ins.then_inc(setup_pe, 1)
            for f in range(FC):
                mm(banks[f // 2][:, f % 2 * D:(f % 2 + 1) * D], a_pj[:, f * P:(f + 1) * P], bt_pj[:], f % 2 == 0, False)
            pe.wait_ge(eff_ready, 2)
            for f in range(FC):
                for c in range(DC):
                    ins = mm(banks[f // 2][:, f % 2 * D + c * P:f % 2 * D + (c + 1) * P],
                             tq2[:, c * F + f * P:c * F + (f + 1) * P], ident[:], False, f % 2 == 1 and c == DC - 1)
                if f % 2 == 1:
                    ins.then_inc(setup_pe, 1)
            pe.sem_inc(pt_full, PT_CREDIT)
            pe.sem_inc(pv_done, PV_CREDIT)

            def unit(k, u):
                if u in FREE_WORK:
                    return
                kind, i = u
                prev, earlier = before(u)
                done, n, place = DONE[prev]
                if not (earlier and isinstance(k, int) and k == 0):
                    pe.wait_ge(done, (k - 1 if earlier else k) * n + place + 1)
                o = psum(u)
                if kind in ("CT", "XT", "ZT"):
                    src, ready, each = {"CT": (up, c_ready, 1), "XT": (x1, x1_ready, NT), "ZT": (y, z_ready, NT)}[kind]
                    if each == 1:
                        pe.wait_ge(ready, k + 1)
                    for t in range(NT):
                        if each > 1:
                            pe.wait_ge(ready, k * NT + t + 1)
                        ins = pe.transpose(o[:, t * P:(t + 1) * P], src[:, t, i * P:(i + 1) * P], ident[:])
                elif kind == "FC":
                    pe.wait_ge(at_ready, k * 3 * DC + DC)
                    for c in range(DC):
                        w = slice(i * P, (i + 1) * P)
                        ins = mm3(o[:], wfc_h[:, c, w], wfc_l[:, c, w], act_h[:, c], act_l[:, c], c == 0, c == DC - 1)
                elif kind == "PJ":
                    pe.wait_ge(h_ready, (k + 1) * FC)
                    tok = slice(i * P, (i + 1) * P)
                    for f in range(FC):
                        ins = mm3(o[:, 0:D], hid_h[:, f, tok], hid_l[:, f, tok], wpj_h[:, f], wpj_l[:, f],
                                  f == 0, f == FC - 1)
                elif kind == "A1":
                    pe.wait_ge(at_ready, k * 3 * DC + 2 * DC)
                    pe.wait_ge(lang_split, k + 1)
                    for b in range(BT):
                        tok = slice(b * S, (b + 1) * S)
                        for c in range(DC):
                            ins = mm3(o[:, tok], w1_h[:, b, c], w1_l[:, b, c], act_h[:, c, tok], act_l[:, c, tok],
                                      c == 0, c == DC - 1)
                elif kind == "A2":
                    pe.wait_ge(rs_ready, k + 1)
                    tok = slice(i * P, (i + 1) * P)
                    mm(o[:, 0:D], rs[:, tok], w2_h[:, i // 2], True, False)
                    ins = mm(o[:, 0:D], rs[:, tok], w2_l[:, i // 2], False, True)
                elif kind == "LG":
                    pe.wait_ge(at_ready, (k + 1) * 3 * DC)
                    for c in range(DC):
                        ins = mm3(o[0:E, :], wg_h[:, c], wg_l[:, c], act_h[:, c], act_l[:, c], c == 0, c == DC - 1)
                elif kind == "LT":
                    pe.wait_ge(lgt_ready, k + 1)
                    settle(pe, "pe")
                    for t in range(NT):
                        ins = pe.transpose(o[:, t * E:(t + 1) * E], lgt[:, t * P:(t + 1) * P], ident[0:E, 0:E])
                elif kind == "V":
                    pe.wait_ge(at_ready, (k + 1) * 3 * DC)
                    tok = slice(i * P, (i + 1) * P)
                    for c in range(DC):
                        ins = mm3(o[:, 0:D], act_h[:, c, tok], act_l[:, c, tok], wv_h[:, c], wv_l[:, c],
                                  c == 0, c == DC - 1)
                elif kind == "QK":
                    pe.wait_ge(at_ready, (k + 1) * 3 * DC)
                    w = slice(i * P, (i + 1) * P)
                    for c in range(DC):
                        ins = mm3(o[:], wqk_h[:, c, w], wqk_l[:, c, w], act_h[:, c], act_l[:, c], c == 0, c == DC - 1)
                elif kind == "CB":
                    pe.wait_ge(comb_ready, k + 1)
                    settle(pe, "pe")
                    for t in range(NT):
                        ins = pe.transpose(o[0:64, t * P:(t + 1) * P], cs[:, t].bitcast(F32), ident[:])
                elif kind == "MB":
                    pe.wait_ge(combt_ready, k + 1)
                    ins = mm(o[:, 0:D], cbt[:, i * P:(i + 1) * P], bex[:])
                else:
                    t, q = divmod(i, 4)
                    tok, e2 = slice(t * P, (t + 1) * P), slice(2 * q, 2 * q + 2)
                    for c in range(DC):
                        ins = mm3(o[:], act_h[:, c, tok], act_l[:, c, tok],
                                  wex_h[:, c, e2].rearrange("p e f -> p (e f)"),
                                  wex_l[:, c, e2].rearrange("p e f -> p (e f)"), c == 0, c == DC - 1)
                ins.then_inc(gen_full, 1)

            def scores(j, n):
                b, h = divmod(n, H)
                if h == 0:
                    pe.wait_ge(qk_loaded[b], 256 * (j + 1))
                if n < 2:
                    done, each, place = DONE[[u for u in EXPERTS if BANK[u] == n][-1]]
                    pe.wait_ge(done, each * j + place + 1)
                pe.wait_ge(p_ready, j * NH + n - 1 + P_CREDIT)
                for qt in range(2):
                    q0 = b * S + qt * P
                    ins = mm(sc[n % 2][:, qt * S:(qt + 1) * S], qs[:, h, q0:q0 + P], ks[:, h, b * S:(b + 1) * S])
                ins.then_inc(s_ready, 1)

            def turn(j, n):
                pe.wait_ge(p_ready, j * NH + n + 1 + P_CREDIT)
                pe.wait_ge(pts_ready, j * NH + n - 1 + PTS_CREDIT)
                for kt in range(2):
                    for qt in range(2):
                        ins = pe.transpose(pt[n % 2][:, kt * S + qt * P:kt * S + (qt + 1) * P],
                                           prob[:, n % 2, qt, kt * P:(kt + 1) * P], ident[:])
                ins.then_inc(pt_full, 1)

            def values(j, n):
                b, h = divmod(n, H)
                g, q = divmod(n, 4)
                pe.wait_ge(pts_ready, j * NH + n + 1 + PTS_CREDIT)
                if q == 0:
                    pe.wait_ge(ot_used, j * NG + g - 1 + OT_CREDIT)
                for kt in range(2):
                    ins = mm(ov[g % 2][32 * q:32 * q + 32, 0:S], val[:, 2 * b + kt, h * VW:h * VW + 32],
                             pts[:, n % 2, kt], kt == 0, kt == 1)
                ins.then_inc(pv_done, 1)

            def turn_back(j, g):
                pe.wait_ge(ovs_ready, j * NG + g + 1)
                for qt in range(2):
                    ins = pe.transpose(ov[g % 2][:, S + qt * P:S + (qt + 1) * P], ovs[:, qt * P:(qt + 1) * P], ident[:])
                ins.then_inc(ot_ready, 1)

            def slots(k, j):
                for n in range(NSLOT):
                    if n < NH:
                        scores(j, n)
                    if 2 <= n < NH + 2:
                        turn(j, n - 2)
                    if 3 <= n < NH + 3:
                        values(j, n - 3)
                    if n >= TURN_BACK and (n - TURN_BACK) % 4 == 0 and (n - TURN_BACK) // 4 < NG:
                        turn_back(j, (n - TURN_BACK) // 4)
                    for step, u in shade(k, j, n):
                        unit(step, u)

            for u in SLOTTED + EXPERTS:
                if u in WEIGHTS_FOR:
                    pe.wait_ge(lo_ready, WEIGHTS_FOR[u])
                if u == ("ME", 0):
                    pe.wait_ge(wex_ready, 1)
                unit(0, u)
            with pe.Fori(1, STEPS) as k:
                slots(k, k - 1)
                for u in EXPERTS:
                    unit(k, u)
            slots(None, STEPS - 1)

        @block.scalar
        def _(act):
            def unit(k, u):
                kind, i = u
                if kind == "W":
                    act.wait_ge(sums_ready, k + 1)
                    for b in range(BT):
                        ins = nc.scalar.activation(up[:, 2 * b:2 * b + 2], x[:, 2 * b:2 * b + 2, 1:D + 1], ACT.Identity,
                                                   scale=z_cur[:, 2, b:b + 1], bias=z_cur[:, 3, b:b + 1])
                    ins.then_inc(w_ready, 1)
                elif kind in ("CT", "XT", "ZT"):
                    full(act, k, u)
                    nc.scalar.activation(act_h[:, i], psum(u)[:], ACT.Copy).then_inc(ah_ready, 1)
                elif kind == "FC":
                    full(act, k, u)
                    wait(act, h_ready, k * FC + i - 1)
                    signal(nc.scalar.activation(gel[:, i % 2], psum(u)[:], ACT.Gelu, bias=bias_cols[:, i:i + 1]), u)
                elif kind == "A1":
                    full(act, k, u)
                    act.wait_ge(lang_loaded, 16 * 18 * (k + 1))
                    for b in range(BT):
                        tok = slice(b * S, (b + 1) * S)
                        ins = nc.scalar.activation(r1[:, tok], psum(u)[:, tok], ACT.Relu, bias=b1c[:, b:b + 1])
                    signal(ins, u)
                elif kind == "QK":
                    full(act, k, u)
                    wait(act, parts_ready, 4 * k + i - 1)
                    for dst in (qk_parts[:, 0, i], qf[:, i % 2]):
                        ins = nc.scalar.activation(dst, psum(u)[:], ACT.Identity, bias=bias_cols[:, 8 + i:9 + i],
                                                   scale=0.25 if i < 2 else 1.0)
                    signal(ins, u)
                elif kind == "LG":
                    full(act, k, u)
                    signal(nc.scalar.activation(lgt[:], psum(u)[0:E, :], ACT.Identity, bias=bg_col[:, 0:1]), u)
                elif u == ("GATE", 0):
                    act.wait_ge(lg_ready, k + 1)
                    nc.scalar.activation(ge[:], lg[:], ACT.Exp).then_inc(ge_ready, 1)
                elif kind == "CB":
                    full(act, k, u)
                    signal(nc.scalar.activation(cbt[:], psum(u)[0:64, :], ACT.Copy), u)

            def exps(j, n):
                act.wait_ge(nm_ready, j * NH + n + 1)
                act.wait_ge(pt_full, j * NH + n - 1 + PT_CREDIT)
                for qt in range(2):
                    ins = nc.scalar.activation(prob[:, n % 2, qt], sc[n % 2][:, qt * S:(qt + 1) * S], ACT.Exp,
                                               bias=nm[:, n % 4, qt:qt + 1])
                ins.then_inc(p_ready, 1)

            def copy_turned(j, n):
                act.wait_ge(pt_full, j * NH + n + 1 + PT_CREDIT)
                act.wait_ge(pv_done, j * NH + n - 1 + PV_CREDIT)
                nc.scalar.activation(pts[:, n % 2].rearrange("p a b -> p (a b)"), pt[n % 2][:], ACT.Copy)\
                    .then_inc(pts_ready, 1)

            def slots(k, j):
                for n in range(NSLOT):
                    if 2 <= n < NH + 2:
                        copy_turned(j, n - 2)
                    if n < NH:
                        exps(j, n)
                    for step, u in shade(k, j, n, LAG_ACT):
                        unit(step, u)

            for half in range(2):
                act.wait_ge(setup_pe, half + 1)
                nc.scalar.activation(bt_fc[:, half * 512:(half + 1) * 512], banks[half][0:R, :], ACT.Copy, scale=2.0)\
                    .then_inc(factors_ready, 1)
            act.wait_ge(setup_pe, 3)
            nc.scalar.activation(bt_pj[:], banks[2][0:R, 0:D], ACT.Copy, scale=2.0).then_inc(factors_ready, 1)
            act.wait_ge(setup_pe, 4)
            nc.scalar.activation(bias_cols[:, 0:8], banks[3][:, 0:8], ACT.Copy)
            nc.scalar.activation(bias_cols[:, 8:10], banks[3][:, 8:10], ACT.Copy, scale=0.25)
            nc.scalar.activation(bias_cols[:, 10:12], banks[3][:, 10:12], ACT.Copy).then_inc(factors_ready, 1)

            def hi(dst, src):
                nc.scalar.activation(dst, src, ACT.Copy).then_inc(hi_ready, 1)

            unit(0, ("W", 0))
            for i in range(4):
                act.wait_ge(setup_pe, 4 + i + 1)
                hi(wfc_h[:, i // 2, i % 2 * 512:(i % 2 + 1) * 512], banks[4 + i][:])
            for i in range(4):
                act.wait_ge(setup_pe, 8 + i + 1)
                hi(wpj_h[:, 2 * i:2 * i + 2], banks[i][:].rearrange("p (f o) -> p f o", f=2))
            act.sem_inc(p_ready, P_CREDIT)
            act.sem_inc(pts_ready, PTS_CREDIT)
            for u in SLOTTED[1:] + EXPERTS:
                unit(0, u)
                if u == ("FC", FC - 1):
                    act.wait_ge(rest_loaded, 64)
                    act.wait_ge(bias_loaded, 16 * 3)
                    hi(wqk_h[:], wqkv_n[:, :, 0:2 * D])
                    hi(wv_h[:], wqkv_n[:, :, 2 * D:3 * D])
                    hi(wg_h[:], wg_n[:])
                    hi(wex_h[:], wex_n[:])
            with act.Fori(1, STEPS) as k:
                slots(k, k - 1)
                for u in EXPERTS:
                    unit(k, u)
            slots(None, STEPS - 1)

        @block.vector
        def _(dve):
            n0 = [0]

            def link0(ins):
                n0[0] += 1
                ins.then_inc(v_step, 1)
                dve.wait_ge(v_step, n0[0])

            for i, w in enumerate((wfc_n, wpj_n)):
                dve.wait_ge(w_loaded[i], 16)
                nc.vector.tensor_reduce(amax[:, i:i + 1], w[:].rearrange("p c d -> p (c d)"), AX.X, ALU.max,
                                        apply_absolute_value=True).then_inc(amax_part, 1)
            dve.wait_ge(z_loaded, 16 * 3)
            link0(nc.vector.tensor_tensor(z_all[:, 3], z_all[:, 0], z_all[:, 1], ALU.add))
            link0(nc.vector.scalar_tensor_tensor(z_all[:, 3], z_all[:, 3], -2.0, z_all[:, 2], ALU.mult, ALU.add))
            nc.vector.tensor_scalar(z_all[:, 2], z_all[:, 2], -1.0, None, ALU.mult).then_inc(z_made, 1)
            for i, (w, q) in enumerate(((wfc_n, tq1), (wpj_n, tq2))):
                dve.wait_ge(amax_all, i + 1)
                m = amax[:, 2 + i:3 + i]
                link0(nc.vector.tensor_scalar(m, m, 1.0 / QMAX, None, ALU.mult))
                link0(nc.vector.reciprocal(amax[:, i:i + 1], m))
                wf = w[:].rearrange("p c d -> p (c d)")
                link0(nc.vector.tensor_scalar(q[:], wf, amax[:, i:i + 1], MAGIC, ALU.mult, ALU.add))
                link0(nc.vector.tensor_scalar(q[:], q[:], MAGIC, QMIN, ALU.subtract, ALU.max))
                link0(nc.vector.tensor_scalar(q[:], q[:], QMAX, m, ALU.min, ALU.mult))
                link0(nc.vector.tensor_tensor(q[:], q[:], wf, ALU.subtract))
                nc.vector.tensor_tensor(q[:], q[:], wf, ALU.add).then_inc(eff_ready, 1)
            dve.wait_ge(consts_made, 1)
            dve.sem_inc(ot_used, OT_CREDIT)

            def low_part(i):
                dve.wait_ge(hi_ready, i + 1)
                if i < 4:
                    c, w = i // 2, slice(i % 2 * 512, (i % 2 + 1) * 512)
                    ins = nc.vector.tensor_tensor(wfc_l[:, c, w], banks[4 + i][:], wfc_h[:, c, w].bitcast(F32), ALU.subtract)
                else:
                    f = slice(2 * (i - 4), 2 * (i - 4) + 2)
                    ins = nc.vector.tensor_tensor(wpj_l[:, f], banks[i - 4][:].rearrange("p (f o) -> p f o", f=2),
                                                  wpj_h[:, f].bitcast(F32), ALU.subtract)
                ins.then_inc(lo_ready, 1)

            def other_weights(part):
                if part == 0:
                    dve.wait_ge(hi_ready, 11)
                    for low, src, high in ((wqk_l[:], wqkv_n[:, :, 0:2 * D], wqk_h[:]),
                                           (wv_l[:], wqkv_n[:, :, 2 * D:3 * D], wv_h[:]),
                                           (wg_l[:], wg_n[:], wg_h[:])):
                        nc.vector.tensor_tensor(low, src, high.bitcast(F32), ALU.subtract).then_inc(lo_ready, 1)
                else:
                    dve.wait_ge(bex_loaded, 64)
                    link0(nc.vector.tensor_copy(bex[:], bex_raw[:]))
                    nc.vector.tensor_tensor(bex[32:64], bex_raw[32:64], bex[32:64].bitcast(F32), ALU.subtract)\
                        .then_inc(lo_ready, 1)


            M_FIRST, M_STEP = 56, 64
            m, m_base = [0], [0]

            def link(ins):
                m[0] += 1
                ins.then_inc(main_step, 1)
                dve.wait_ge(main_step, m_base[0] + m[0])

            def unit(k, u):
                kind, i = u
                o = None if u in FREE_WORK else psum(u)
                if kind == "ST":
                    dve.wait_ge(wx_ready, k + 1)
                    for b in range(BT):
                        ts = slice(2 * b, 2 * b + 2)
                        ins = nc.vector.scalar_tensor_tensor(up[:, ts], (lap, dn)[i][:, ts], z_cur[:, i, b:b + 1],
                                                             up[:, ts], ALU.mult, ALU.add)
                    if i == 0:
                        link(ins)
                    else:
                        ins.then_inc(c_ready, 1)
                elif kind == "SPLIT":
                    split_languages(k)
                elif kind == "LN":
                    normalize(k, i)
                elif kind == "LT":
                    full(dve, k, u)
                    signal(nc.vector.tensor_copy(lg[:], o[:, 0:NT * E].rearrange("p (t e) -> p t e", e=E)), u)
                    dve.wait_ge(logits_made, k + 1)
                    gate_shift()
                elif kind == "GATE":
                    gate(k, i)
                elif kind in ("CT", "XT", "ZT"):
                    dve.wait_ge(ah_ready, DONE[u][1] * k + DONE[u][2] + 1)
                    signal(nc.vector.tensor_tensor(act_l[:, i], o[:], act_h[:, i].bitcast(F32), ALU.subtract), u)
                elif kind == "FC":
                    dve.wait_ge(g_ready, k * FC + i + 1)
                    link(nc.vector.tensor_copy(hid_h[:, i], gel[:, i % 2]))
                    nc.vector.tensor_tensor(hid_l[:, i], gel[:, i % 2], hid_h[:, i].bitcast(F32), ALU.subtract)\
                        .then_inc(h_ready, 1)
                elif kind == "PJ":
                    full(dve, k, u)
                    dve.wait_ge(xb_ready, k + 1)
                    signal(nc.vector.tensor_tensor(x1[:, i], o[:, 0:D], x[:, i, 1:D + 1], ALU.add), u)
                elif kind == "A1":
                    dve.wait_ge(r1_ready, k + 1)
                    link(nc.vector.tensor_copy(rs[:], r1[:]))
                    nc.vector.tensor_tensor(rs[A:P], r1[A:P], rs[A:P].bitcast(F32), ALU.subtract).then_inc(rs_ready, 1)
                elif kind == "A2":
                    full(dve, k, u)
                    dve.wait_ge(xb2_ready, k * NT + i + 1)
                    signal(nc.vector.tensor_tensor(y[:, i], o[:, 0:D], xb2[:, i], ALU.add), u)
                    if i >= 1:
                        stats(k, i - 1)
                    if i >= 2:
                        moments(k, i - 2)
                    if i >= 3:
                        center(k, i - 3)
                elif kind == "V":
                    full(dve, k, u)
                    signal(nc.vector.tensor_tensor(val[:, i, 0:H * VW].rearrange("p (h w) -> p h w", w=VW)[:, :, 0:HD],
                                                   o[:, 0:D].rearrange("p (h d) -> p h d", d=HD),
                                                   bv_bc[:].rearrange("p (h d) -> p h d", d=HD), ALU.add), u)
                elif kind == "QK":
                    dve.wait_ge(qf_ready, 4 * k + i + 1)
                    q = qf[:, i % 2]
                    link(nc.vector.tensor_tensor(q, q, qk_parts[:, 0, i], ALU.subtract))
                    link(nc.vector.tensor_copy(qk_parts[:, 1, i], q))
                    nc.vector.tensor_tensor(qk_parts[:, 2, i], q, qk_parts[:, 1, i], ALU.subtract)\
                        .then_inc(parts_ready, 1)
                elif kind == "MB":
                    full(dve, k, u)
                    late = i >= NT // BT
                    if late:
                        wait(dve, stored[i // 2], 16 * k)
                    else:
                        dve.wait_ge(moe_added, DONE[u][1] * k + DONE[u][2] - 1)
                    signal(nc.vector.tensor_tensor(acc[:, i], o[:, 0:D], x1[:, i] if late else acc[:, i], ALU.add), u)
                elif kind == "ME":
                    t, q = divmod(i, 4)
                    if u in LATE_EXPERTS:
                        experts(k, [u], q)
                    elif t % 2 == 1:
                        experts(k, [("ME", i - 4), u], q)

            def experts(k, pair, q):
                early = pair[0] in EXPERTS
                for u in pair:
                    full(dve, k, u)
                    if q == 0 and early:
                        wait(dve, stored[0], 16 * k)
                    elif q == 0:
                        dve.wait_ge(moe_added, DONE[pair[0]][1] * k + DONE[pair[0]][2])
                    else:
                        dve.wait_ge(moe_added, DONE[u][1] * k + DONE[u][2] - 1)
                    t = u[1] // 4
                    nc.vector.scalar_tensor_tensor(acc[:, t], psum(u)[:, 0:D], cmb[:, t, 2 * q:2 * q + 1],
                                                   x1[:, t] if early and q == 0 else acc[:, t], ALU.mult, ALU.add)\
                        .then_inc(main_step, 1)
                for n, u in enumerate(pair):
                    t = u[1] // 4
                    m[0] += 1
                    dve.wait_ge(main_step, m_base[0] + m[0])
                    signal(nc.vector.scalar_tensor_tensor(acc[:, t], psum(u)[:, D:2 * D], cmb[:, t, 2 * q + 1:2 * q + 2],
                                                          acc[:, t], ALU.mult, ALU.add), u)

            def wide(v):
                return v.unsqueeze(2).to_broadcast([P, NT, E])

            def gate_shift():
                link(nc.vector.tensor_reduce(gm[:], lg[:], AX.X, ALU.max))
                nc.vector.tensor_tensor(lg[:], lg[:], wide(gm[:]), ALU.subtract).then_inc(lg_ready, 1)

            def gate_top(g, s):
                link(nc.vector.tensor_reduce(gm[:], g[:], AX.X, ALU.max))
                link(nc.vector.tensor_tensor(eq[:], g[:], wide(gm[:]), ALU.is_equal))
                link(nc.vector.tensor_tensor(eq[:], eq[:], rank_row[:].unsqueeze(1).to_broadcast([P, NT, E]), ALU.mult))
                link(nc.vector.tensor_reduce(gm[:], eq[:], AX.X, ALU.max))
                link(nc.vector.tensor_tensor(s[:], eq[:], wide(gm[:]), ALU.is_equal))

            def gate(k, i):
                if i == 0:
                    dve.wait_ge(ge_ready, k + 1)
                    link(nc.vector.tensor_reduce(gm[:], ge[:], AX.X, ALU.add))
                    link(nc.vector.reciprocal(gm[:], gm[:]))
                    link(nc.vector.tensor_tensor(gt[:], ge[:], wide(gm[:]), ALU.mult))
                elif i == 1:
                    gate_top(gt, s1)
                    link(nc.vector.scalar_tensor_tensor(g2[:], s1[:], -2.0, gt[:], ALU.mult, ALU.add))
                elif i == 2:
                    gate_top(g2, s2)
                    link(nc.vector.tensor_tensor(s1[:], s1[:], s2[:], ALU.add))
                    link(nc.vector.tensor_tensor(cmb[:], s1[:], gt[:], ALU.mult))
                else:
                    nc.vector.tensor_copy(cs[:, :, 0:E], cmb[:])
                    link(nc.vector.tensor_copy(cs[:, :, 32:32 + E], cmb[:]))
                    for at in (E, 32 + E):
                        ins = nc.vector.tensor_tensor(cs[:, :, at:at + E], cmb[:], cs[:, :, 0:E].bitcast(F32), ALU.subtract)
                    ins.then_inc(comb_ready, 1)

            def split_languages(k):
                dve.wait_ge(lang_loaded, 16 * 18 * (k + 1))
                w1 = wraw[:, 0].rearrange("p b (c m) -> p b c m", c=DC)
                nc.vector.tensor_copy(w1_h[:], w1)
                link(nc.vector.tensor_copy(w2_h[:], wraw[:, 1]))
                nc.vector.tensor_tensor(w1_l[:], w1, w1_h[:].bitcast(F32), ALU.subtract)
                nc.vector.tensor_tensor(w2_l[:], wraw[:, 1], w2_h[:].bitcast(F32), ALU.subtract).then_inc(lang_split, 1)

            def stats(k, t):
                dve.wait_ge(y_ready, k * NT + t + 1)
                nc.vector.bn_stats(st[:, t], y[:, t]).then_inc(st_ready, 1)

            def moments(k, t):
                dve.wait_ge(st_ready, k * NT + t + 1)
                settle(dve, "dve")
                nc.vector.bn_aggr(mv[:, t], st[:, t]).then_inc(mv_ready, 1)

            def center(k, t):
                dve.wait_ge(mv_ready, k * NT + t + 1)
                nc.vector.scalar_tensor_tensor(y[:, t], y[:, t], mv[:, t, 0:1], bc[:, t // 2, 1],
                                               ALU.subtract, ALU.mult).then_inc(centered, 1)

            def normalize(k, i):
                if i == 0:
                    stats(k, NT - 1)
                    moments(k, NT - 2)
                    center(k, NT - 3)
                    moments(k, NT - 1)
                    center(k, NT - 2)
                    dve.wait_ge(mv_ready, (k + 1) * NT)
                    link(nc.vector.tensor_scalar(ve[:], mv[:, :, 1], LN_EPS, None, ALU.add))
                    center(k, NT - 1)
                    link(nc.vector.tensor_scalar(rsd[:].bitcast(I32), ve[:].bitcast(I32), -0.5, RSQRT_SEED,
                                                 ALU.mult, ALU.add))
                elif i <= NEWTON:
                    link(nc.vector.scalar_tensor_tensor(rst[:], rsd[:], -0.5, rsd[:], ALU.mult, ALU.mult))
                    link(nc.vector.tensor_tensor(rst[:], rst[:], ve[:], ALU.mult))
                    link(nc.vector.scalar_tensor_tensor(rsd[:], rst[:], 1.5, rsd[:], ALU.add, ALU.mult))
                else:
                    dve.wait_ge(centered, (k + 1) * NT)
                    for t in range(NT):
                        nc.vector.scalar_tensor_tensor(y[:, t], y[:, t], rsd[:, t:t + 1], bc[:, t // 2, 2],
                                                       ALU.mult, ALU.add).then_inc(z_ready, 1)

            A_STEP = NG
            s = [0]

            def alink(j, ins):
                s[0] += 1
                ins.then_inc(att_step, 1)
                dve.wait_ge(att_step, j * A_STEP + s[0])

            def slots(k, j):
                s[0] = 0
                for n in range(NSLOT):
                    if n >= 7 and n % 4 == 3:
                        g = (n - 7) // 4
                        dve.wait_ge(pv_done, j * NH + 4 * g + 4 + PV_CREDIT)
                        nc.vector.tensor_copy(ovs[:], ov[g % 2][:, 0:S]).then_inc(ovs_ready, 1)
                    if n < NH:
                        dve.wait_ge(s_ready, j * NH + n + 1)
                        nc.vector.tensor_reduce(nm[:, n % 4], sc[n % 2][:].rearrange("p (q k) -> p q k", q=2), AX.X,
                                                ALU.max, negate=True).then_inc(nm_ready, 1)
                    if n >= NORM and (n - NORM) % 4 == 0:
                        g = (n - NORM) // 4
                        b, gb = divmod(g, NG // BT)
                        dve.wait_ge(ot_ready, j * NG + g + 1)
                        o = ov[g % 2][:, S:2 * S].rearrange("p (q h w) -> p q h w", q=2, h=4)
                        alink(j, nc.vector.reciprocal(rden[:], o[:, :, :, HD:VW]))
                        nc.vector.tensor_tensor(tmp[:], o[:, :, :, 0:HD], rden[:].to_broadcast([P, 2, 4, HD]),
                                                ALU.mult).then_inc(ot_used, 1)
                        dve.wait_ge(ot_used, j * NG + g + 1 + OT_CREDIT)
                        dst = acc[:, 2 * b:2 * b + 2, gb * 4 * HD:(gb + 1) * 4 * HD]
                        nc.vector.tensor_tensor(dst, dst, tmp[:].rearrange("p q h w -> p q (h w)"), ALU.add)\
                            .then_inc(att_added, 1)
                    for step, u in shade(k, j, n, LAG_DVE):
                        unit(step, u)

            for i in range(4):
                low_part(i)
            for u in SLOTTED + EXPERTS:
                unit(0, u)
                if u == ("CT", 1):
                    for i in range(4, 8):
                        low_part(i)
                elif u == ("PJ", 0):
                    other_weights(0)
                elif u == ("PJ", 3):
                    other_weights(1)
            assert m[0] == M_FIRST, f"{m[0]} steps"
            with dve.Fori(1, STEPS) as k:
                m[0], m_base[0] = 0, (k - 1) * M_STEP + M_FIRST
                slots(k, k - 1)
                for u in EXPERTS:
                    unit(k, u)
                assert m[0] == M_STEP, f"{m[0]} steps"
            m[0], m_base[0] = 0, (STEPS - 1) * M_STEP + M_FIRST
            slots(None, STEPS - 1)


_INS = ["x", "condB_zX", "condB_zY", "condB_zR", "itok_B_0_8", "L0_ffn_W_fc", "L0_ffn_b_fc", "L0_ffn_A_fc",
        "L0_ffn_B_fc", "L0_ffn_W_proj", "L0_ffn_b_proj", "L0_ffn_A_proj", "L0_ffn_B_proj", "L1_cond_W1",
        "L1_cond_b1", "L1_cond_W2", "L1_cond_b2", "L1_cond_gamma", "L1_cond_beta", "L1_ffn_W_qkv",
        "L1_ffn_b_qkv", "L1_ffn_W_gate", "L1_ffn_b_gate", "L1_ffn_W_experts", "L1_ffn_b_experts"]


def kernel(**inputs):
    import numpy as np
    import concourse.bacc as bacc
    from concourse.bass_utils import run_bass_kernel_spmd

    nc = bacc.Bacc("TRN2", target_bir_lowering=False, num_devices=1)
    arrays, aps = {}, {}
    for name in _INS:
        v = np.ascontiguousarray(inputs[name])
        arrays[f"in_{name}"] = v
        aps[name] = nc.dram_tensor(f"in_{name}", v.shape, mybir.dt.from_np(v.dtype), kind="ExternalInput").ap()
    out = nc.dram_tensor("out", (B, S, D), F32, kind="ExternalOutput").ap()
    block_kernel(nc, aps, out)
    return run_bass_kernel_spmd(nc, [arrays], core_ids=[0]).results[0]["out"]
```

```python
from contextlib import ExitStack

import concourse.bass as bass
from concourse import mybir

ALU = mybir.AluOpType
ACT = mybir.ActivationFunctionType
AX = mybir.AxisListType
F32 = mybir.dt.float32
F32R = mybir.dt.float32r
BF16 = mybir.dt.bfloat16
I32 = mybir.dt.int32

P = 128
B, S, D = 16, 256, 256
F = 1024
H, HD = 16, 16
E = 8
A = 64
R = 16
L = 10

BT = 2
TOK = BT * S
STEPS = B // BT
NT = TOK // P
DC = D // P
FC = F // P
NH = BT * H
NG = NH // 4
VW = HD + 1
QMAX, QMIN = 127.0, -128.0
MAGIC = 1.5 * 2.0**23
LN_EPS = 1e-5
RSQRT_SEED = 1597463007.0

Q_PART = (0, 0, 1, 1, 0, 2, 1, 2)
K_PART = (0, 1, 0, 1, 2, 0, 2, 1)

NEWTON = 3
FREE_WORK = [("W", 0), ("ST", 0), ("ST", 1), ("SPLIT", 0)] + [("LN", i) for i in range(NEWTON + 2)] + [("EXP", 0)]
SLOTTED = (
    [("W", 0), ("ST", 0), ("ST", 1)]
    + [("CT", c) for c in range(DC)]
    + [("FC", f) for f in range(FC)]
    + [("PJ", 0), ("PJ", 1), ("SPLIT", 0), ("PJ", 2), ("PJ", 3)]
    + [("XT", c) for c in range(DC)]
    + [("A1", 0)]
    + [("A2", t) for t in range(NT)]
    + [("LN", i) for i in range(NEWTON + 2)]
    + [("ZT", c) for c in range(DC)]
    + [("LG", 0)]
    + [("QK", 0), ("LT", 0), ("EXP", 0), ("QK", 1), ("QK", 2), ("QK", 3)]
    + [("V", t) for t in range(NT)]
)
CB_AT, MB_AT = 3, 8
EXPERTS = [("ME", 4 * t + q) for q in range(4) for t in range(NT // BT)]
EXPERTS = EXPERTS[:CB_AT] + [("CB", 0)] + EXPERTS[CB_AT:MB_AT] + [("MB", t) for t in range(NT)] + EXPERTS[MB_AT:]
LATE_EXPERTS = [("ME", 4 * t + q) for q in range(4) for t in range(NT // BT, NT)]
ADDS = [u for u in EXPERTS + LATE_EXPERTS if u != ("CB", 0)]
UNITS = [u for u in SLOTTED + EXPERTS + LATE_EXPERTS if u not in FREE_WORK]
NU = len(UNITS)
SHADE = {
    "W": [2], "ST": [5, 6], "CT": [7, 7], "FC": [9] * 8,
    "PJ": [11, 13, 14, 14], "SPLIT": [14], "XT": [14, 14],
    "A1": [17], "A2": [19, 19, 20, 20], "LN": [20] * 5, "ZT": [21, 21],
    "LG": [24], "QK": [25, 28, 30, 30], "LT": [27], "EXP": [27],
    "V": [32, 33, 35, 37],
}
LATE_SLOTS = (1, 1, 2, 2, 2, 3, 3, 4)
LAG_ACT, LAG_DVE = {"PJ": 1, "A2": 1}, {"XT": 1, "QK": 1, "ZT": 1, "CT": 1, "A1": 1}
SLOT = {(kind, i): n for kind, at in SHADE.items() for i, n in enumerate(at)}
LAST_LATE_SLOTS = (0, 1, 3, 5, 7, 9, 11, 13)
TURN_BACK, NORM = 8, 9
NSLOT = NH - 4 + NORM + 1
BANK = {}
for _i, _u in enumerate(u for u in UNITS if u in SLOTTED):
    BANK[_u] = 6 + _i % 2
for _i, _u in enumerate(EXPERTS):
    BANK[_u] = (7, 0, 1, 6)[_i % 4]
for _i, _u in enumerate(LATE_EXPERTS):
    BANK[_u] = 6 + _i % 2


def before(u):
    at = UNITS.index(u)
    for i in range(at - 1, at - NU - 1, -1):
        if BANK[UNITS[i]] == BANK[u]:
            return UNITS[i], i < 0


def shade(k, j, n, lag={}):
    for u, at in zip(LATE_EXPERTS, LATE_SLOTS if k is not None else LAST_LATE_SLOTS):
        if at + lag.get(u[0], 0) == n:
            yield j, u
    for u in SLOTTED if k is not None else []:
        if SLOT[u] + lag.get(u[0], 0) == n:
            yield k, u


def wait(eng, sem, value):
    if isinstance(value, int) and value <= 0:
        return
    eng.wait_ge(sem, value)


def block_kernel(nc, a, out):
    scr = nc.dram_tensor("qk_parts", (2, 3, D, TOK), BF16, kind="Internal").ap()
    ctx = ExitStack()
    with ctx:
        top = [(nc.sbuf_base + 63) // 64 * 64]

        def sb(name, shape, dt=F32, at=None):
            n = 1
            for s in shape[1:]:
                n *= s
            n = (n * (2 if dt == BF16 else 4) + 63) // 64 * 64
            if at is None:
                at = top[0]
                top[0] += n
            t = nc.alloc_sbuf_tensor_at(name, shape, dt, offset=at)
            return t

        def region(nbytes):
            at = top[0]
            top[0] += nbytes
            return at

        def sem(name):
            return ctx.enter_context(nc.semaphore(name))

        ident = sb("ident", [P, P])
        wfc_h, wfc_l = sb("wfc_h", [P, DC, F], F32R), sb("wfc_l", [P, DC, F], F32R)
        wpj_h, wpj_l = sb("wpj_h", [P, FC, D], F32R), sb("wpj_l", [P, FC, D], F32R)
        wqk_h, wqk_l = sb("wqk_h", [P, DC, 2 * D], F32R), sb("wqk_l", [P, DC, 2 * D], F32R)
        wv_h, wv_l = sb("wv_h", [P, DC, D], F32R), sb("wv_l", [P, DC, D], F32R)
        wg_h, wg_l = sb("wg_h", [P, DC, E], F32R), sb("wg_l", [P, DC, E], F32R)
        wex_h, wex_l = sb("wex_h", [P, DC, E, D], F32R), sb("wex_l", [P, DC, E, D], F32R)
        bex = sb("bex", [64, D], F32R)
        bias_cols = sb("bias_cols", [P, 12])
        bpj_bc = sb("bpj_bc", [P, D])
        bv_bc, bg_col = sb("bv_bc", [P, D]), sb("bg_col", [E, 1])
        rank_row = sb("rank_row", [P, E])
        z_all = sb("z_all", [P, 4, B])
        z_cur = sb("z_cur", [P, 4, BT])

        h_at = region(2 * FC * TOK * 4)
        hid_h = sb("hid_h", [P, FC, TOK], F32R, at=h_at)
        hid_l = sb("hid_l", [P, FC, TOK], F32R, at=h_at + FC * TOK * 4)
        qk_parts = sb("qk_parts_sb", [P, 3, 4, TOK], BF16, at=h_at)
        qk_at = region(2 * H * TOK * 2)
        qs = sb("qs", [P, H, TOK], BF16, at=qk_at)
        ks = sb("ks", [P, H, TOK], BF16, at=qk_at + H * TOK * 2)
        act_h, act_l = sb("act_h", [P, DC, TOK], F32R), sb("act_l", [P, DC, TOK], F32R)
        x = sb("x", [P, NT, D + 2])
        u_at, d_at, t_at = region(4096), region(4096), region(4096)
        up = sb("up", [P, NT, D], at=u_at)
        wraw = sb("wraw", [P, 2, BT, D], at=u_at)
        y = sb("y", [P, NT, D], at=u_at)
        dn = sb("dn", [P, NT, D], at=d_at)
        xb2 = sb("xb2", [P, NT, D], at=d_at)
        lap = sb("lap", [P, NT, D], at=t_at)
        gel = sb("gel", [P, 2, TOK], at=t_at)
        qf = sb("qf", [P, 2, TOK], at=t_at)
        r1 = sb("r1", [P, TOK], at=t_at)
        rs = sb("rs", [P, TOK], F32R, at=t_at + TOK * 4)
        lgt = sb("lgt", [E, TOK], at=t_at + TOK * 4)
        zt = sb("zt", [P, DC, TOK], at=t_at)
        x1 = sb("x1", [P, NT, D])
        acc = sb("acc", [P, NT, D])
        val = sb("val", [P, NT, H * VW + 16])
        p_at, pts_at = region(4096), region(4096)
        prob = sb("prob", [P, 2, 2, S], at=p_at)
        pts = sb("pts", [P, 2, 2, S], at=pts_at)
        ovs = sb("ovs", [P, S])
        tmp = sb("tmp", [P, 2, 4, HD])
        rden = sb("rden", [P, 2, 4, 1])
        nm = sb("nm", [P, 4, 2])
        b2_bc = sb("b2_bc", [P, BT, D])
        gb = sb("gb", [P, BT, 2, DC])
        w1_h, w1_l = sb("w1_h", [P, BT, DC, P], F32R), sb("w1_l", [P, BT, DC, P], F32R)
        w2_h, w2_l = sb("w2_h", [P, BT, D], F32R), sb("w2_l", [P, BT, D], F32R)
        b1c = sb("b1c", [P, BT])
        st = sb("st", [P, NT, 6])
        mv = sb("mv", [P, NT, 2])
        ve, rsd, rst = sb("ve", [P, NT]), sb("rsd", [P, NT]), sb("rst", [P, NT])
        lg, ge, gt, g2 = (sb(n, [P, NT, E]) for n in ("lg", "ge", "gt", "g2"))
        eq, s1, s2, cmb = (sb(n, [P, NT, E]) for n in ("eq", "s1", "s2", "cmb"))
        gm = sb("gm", [P, NT])
        cs = sb("cs", [P, NT, 64], F32R)
        cbt = sb("cbt", [64, TOK], F32R, at=pts_at)
        amax = sb("amax", [P, 4])
        assert top[0] <= nc.sbuf_base + 212863, top[0]

        wfc_n = sb("wfc_n", [P, FC, D], at=h_at)
        wpj_n = sb("wpj_n", [P, DC, F], at=h_at + 8192)
        tq1 = sb("tq1", [P, 2048], at=h_at + 16384)
        tq2 = sb("tq2", [P, 2048], at=h_at + 24576)
        wex_n = sb("wex_n", [P, DC, E, D], at=qk_at)
        wqkv_n = sb("wqkv_n", [P, DC, 3 * D], at=qk_at + 16384)
        wg_n = sb("wg_n", [P, DC, E], at=qk_at + 22528)
        a_fc = sb("a_fc", [R, D], at=qk_at + 22592)
        b_fcn = sb("b_fcn", [P, FC, R], at=qk_at + 23616)
        b_pjn = sb("b_pjn", [P, DC, R], at=qk_at + 24128)
        bt_pj = sb("bt_pj", [R, D], at=qk_at + 24256)
        bias_rows = sb("bias_rows", [12, P], at=qk_at + 25600)
        bex_raw = sb("bex_raw", [64, D], at=qk_at + 26112)
        bt_fc = sb("bt_fc", [R, F], at=p_at)
        a_pj = sb("a_pj", [R, F], at=pts_at)

        banks = [ctx.enter_context(nc.psum_tensor(f"bank{i}", [P, 512], F32)) for i in range(8)]
        sc = banks[0:2]
        pt = banks[2:4]
        ov = banks[4:6]

        w_loaded = [sem(f"w_loaded{i}") for i in range(2)]
        z_loaded = sem("z_loaded")
        factors_ready = sem("factors_ready")
        lo_ready = sem("lo_ready")
        wex_ready = sem("wex_ready")
        z_made = sem("z_made")
        lora_loaded = sem("lora_loaded")
        rest_loaded = sem("rest_loaded")
        bias_loaded = sem("bias_loaded")
        bex_loaded = sem("bex_loaded")
        bex_zeroed = sem("bex_zeroed")
        ident_made = sem("ident_made")
        consts_made = sem("consts_made")
        amax_part = sem("amax_part")
        amax_all = sem("amax_all")
        setup_pe = sem("setup_pe")
        eff_ready = sem("eff_ready")
        hi_ready = sem("hi_ready")
        v_step = sem("v_step")
        p_step = sem("p_step")

        first_x_loaded = sem("first_x_loaded")
        x_loaded = sem("x_loaded")
        c_ready = sem("c_ready")
        xb_ready = sem("xb_ready")
        sums_ready = sem("sums_ready")
        w_ready = sem("w_ready")
        wx_ready = sem("wx_ready")
        ah_ready = sem("ah_ready")
        at_ready = sem("at_ready")
        g_ready = sem("g_ready")
        h_ready = sem("h_ready")
        x1_ready = sem("x1_ready")
        xb2_ready = sem("xb2_ready")
        lang_loaded = sem("lang_loaded")
        lang_split = sem("lang_split")
        r1_ready = sem("r1_ready")
        rs_ready = sem("rs_ready")
        y_ready = sem("y_ready")
        st_ready = sem("st_ready")
        mv_ready = sem("mv_ready")
        z_ready = sem("z_ready")
        v_ready = sem("v_ready")
        qk_high_ready = sem("qk_high_ready")
        qf_ready = sem("qf_ready")
        parts_ready = sem("parts_ready")
        scr_written = sem("scr_written")
        qk_loaded = [sem(f"qk_loaded{b}") for b in range(BT)]
        lgt_ready = sem("lgt_ready")
        logits_made = sem("logits_made")
        lg_ready = sem("lg_ready")
        ge_ready = sem("ge_ready")
        gate_step = sem("gate_step")
        qk_mid_ready = sem("qk_mid_ready")
        combt_ready = sem("combt_ready")
        moe_added = sem("moe_added")
        gen_full = sem("gen_full")
        main_step = sem("main_step")
        att_step = sem("att_step")

        s_ready = sem("s_ready")
        nm_ready = sem("nm_ready")
        p_ready = sem("p_ready")
        pt_full = sem("pt_full")
        pts_ready = sem("pts_ready")
        pv_done = sem("pv_done")
        ovs_ready = sem("ovs_ready")
        ot_ready = sem("ot_ready")
        ot_used = sem("ot_used")
        att_added = sem("att_added")
        stored = [sem(f"stored{b}") for b in range(BT)]

        settled = {n: sem(f"settled_{n}") for n in ("sp", "pool", "pe", "dve")}

        def settle(eng, name):
            eng.sem_inc(settled[name], 1)

        WEIGHTS_FOR = {("CT", 0): 4, ("PJ", 0): 8, ("LG", 0): 11, ("MB", 0): 12}

        GATE_STEPS = 20
        GATE_AT = {("QK", 0): ((), (), ()), ("QK", 1): ((0,), (1,), (2, 3)), ("QK", 2): ((4,), (5,), (6, 7)),
                   ("QK", 3): ((8,), (9,), (10, 11)), ("V", 0): (12, 13), ("V", 1): (14, 15), ("V", 2): (16, 17),
                   ("V", 3): (18, 19)}

        DONE = {}
        for c in range(DC):
            DONE[("CT", c)] = (at_ready, 3 * DC, c)
            DONE[("XT", c)] = (at_ready, 3 * DC, DC + c)
            DONE[("ZT", c)] = (at_ready, 3 * DC, 2 * DC + c)
        for f in range(FC):
            DONE[("FC", f)] = (g_ready, FC, f)
        for t in range(NT):
            DONE[("PJ", t)] = (x1_ready, NT, t)
            DONE[("A2", t)] = (y_ready, NT, t)
            DONE[("V", t)] = (v_ready, NT, t)
            DONE[("QK", t)] = (qf_ready, 4, t)
        DONE[("A1", 0)] = (r1_ready, 1, 0)
        for i, u in enumerate(ADDS):
            DONE[u] = (moe_added, len(ADDS), i)
        DONE[("LG", 0)] = (lgt_ready, 1, 0)
        DONE[("LT", 0)] = (logits_made, 1, 0)
        DONE[("CB", 0)] = (combt_ready, 1, 0)

        def full(eng, k, unit):
            eng.wait_ge(gen_full, k * NU + UNITS.index(unit) + 1)

        def signal(ins, unit):
            ins.then_inc(DONE[unit][0], 1)

        def psum(unit):
            return banks[BANK[unit]]

        P_CREDIT, PT_CREDIT, PTS_CREDIT, PV_CREDIT, OT_CREDIT = 2, 2, 2, 2, 2

        block = ctx.enter_context(nc.Block())

        def load_x(eng, xs, loaded):
            for b in range(BT):
                eng.dma_start(x[:, 2 * b:2 * b + 2, 1:D + 1],
                              xs[b].rearrange("(t p) d -> p t d", p=P)).then_inc(loaded, 16)

        def load_rows(eng, xs, loaded):
            for b in range(BT):
                t0, t1 = 2 * b, 2 * b + 1
                eng.dma_start(up[1:P, t0], xs[b, 0:P - 1]).then_inc(loaded, 16)
                eng.dma_start(up[0:1, t0], xs[b, 1:2]).then_inc(loaded, 16)
                eng.dma_start(up[:, t1], xs[b, P - 1:2 * P - 1]).then_inc(loaded, 16)
                eng.dma_start(dn[:, t0], xs[b, 1:P + 1]).then_inc(loaded, 16)
                eng.dma_start(dn[0:P - 1, t1], xs[b, P + 1:2 * P]).then_inc(loaded, 16)
                eng.dma_start(dn[P - 1:P, t1], xs[b, 2 * P - 2:2 * P - 1]).then_inc(loaded, 16)

        @block.sync
        def _(sp):
            sp.dma_start(wfc_n[:], a["L0_ffn_W_fc"].rearrange("(c p) d -> p c d", p=P)).then_inc(w_loaded[0], 16)
            sp.dma_start(b_fcn[:], a["L0_ffn_B_fc"].rearrange("(c p) r -> p c r", p=P)).then_inc(lora_loaded, 16)
            sp.dma_start(b_pjn[:], a["L0_ffn_B_proj"].rearrange("(c p) r -> p c r", p=P)).then_inc(lora_loaded, 16)
            sp.dma_start(wpj_n[:], a["L0_ffn_W_proj"].rearrange("(c p) f -> p c f", p=P)).then_inc(w_loaded[1], 16)
            sp.dma_start(a_fc[:], a["L0_ffn_A_fc"]).then_inc(lora_loaded, 16)
            sp.dma_start(a_pj[:], a["L0_ffn_A_proj"]).then_inc(lora_loaded, 16)
            sp.dma_start(bias_rows[0:8, :], a["L0_ffn_b_fc"].rearrange("(c p) -> c p", p=P)).then_inc(lora_loaded, 16)
            sp.dma_start(bias_rows[8:12, :], a["L1_ffn_b_qkv"][0:2 * D].rearrange("(c p) -> c p", p=P))\
                .then_inc(lora_loaded, 16)
            for i, n in enumerate(("condB_zX", "condB_zY", "condB_zR")):
                sp.dma_start(z_all[:, i, :], a[n].partition_broadcast(P)).then_inc(z_loaded, 16)
            load_x(sp, a["x"][0:BT], first_x_loaded)
            load_rows(sp, a["x"][0:BT], first_x_loaded)
            for dst, src in ((bpj_bc[:], a["L0_ffn_b_proj"]), (bv_bc[:], a["L1_ffn_b_qkv"][2 * D:3 * D])):
                sp.dma_start(dst, src.partition_broadcast(P)).then_inc(bias_loaded, 16)
            with nc.allow_non_contiguous_dma(reason="one bias for each partition"):
                sp.dma_start(bg_col[:], a["L1_ffn_b_gate"].rearrange("(e o) -> e o", o=1)).then_inc(bias_loaded, 16)
            sp.dma_start(wqkv_n[:], a["L1_ffn_W_qkv"].rearrange("(c p) n -> p c n", p=P)).then_inc(rest_loaded, 16)
            sp.dma_start(wg_n[:], a["L1_ffn_W_gate"].rearrange("(c p) n -> p c n", p=P)).then_inc(rest_loaded, 16)
            for c in range(DC):
                sp.dma_start(wex_n[:, c], a["L1_ffn_W_experts"][:, c * P:(c + 1) * P, :].rearrange("e p f -> p e f"))\
                    .then_inc(rest_loaded, 16)
            sp.wait_ge(bex_zeroed, 1)
            for r in (0, 8, 32, 40):
                sp.dma_start(bex_raw[r:r + E, :], a["L1_ffn_b_experts"]).then_inc(bex_loaded, 16)

            def languages(k):
                sp.wait_ge(at_ready, k * 3 * DC + DC)
                settle(sp, "sp")
                for b in range(BT):
                    lang = sp.value_load(a["itok_B_0_8"].rearrange("(o n) -> o n", o=1)[:, bass.ds(k * BT + b, 1)],
                                         min_val=0, max_val=L - 1)
                    w1 = a["L1_cond_W1"][bass.ds(lang, 1)].rearrange("l (c p) a -> p (l c) a", p=P)
                    w2 = a["L1_cond_W2"][bass.ds(lang, 1)].rearrange("l a h -> (l a) h")
                    b1 = a["L1_cond_b1"][bass.ds(lang, 1)].rearrange("l a -> a l")
                    for half in range(2):
                        w1_half = wraw[:, 0, b].rearrange("p (c m) -> p c m", c=DC)[:, :, half * A:(half + 1) * A]
                        sp.dma_start(w1_half, w1).then_inc(lang_loaded, 16)
                        sp.dma_start(wraw[half * A:(half + 1) * A, 1, b], w2).then_inc(lang_loaded, 16)
                        with nc.allow_non_contiguous_dma(reason="one value for each partition"):
                            sp.dma_start(b1c[half * A:(half + 1) * A, b:b + 1], b1).then_inc(lang_loaded, 16)
                    with nc.allow_non_contiguous_dma(reason="one value for each partition"):
                        for i, n in enumerate(("L1_cond_gamma", "L1_cond_beta")):
                            sp.dma_start(gb[:, b, i], a[n][bass.ds(lang, 1)].rearrange("l (c p) -> p (l c)", p=P))\
                                .then_inc(lang_loaded, 16)
                    sp.dma_start(b2_bc[:, b], a["L1_cond_b2"][bass.ds(lang, 1)].rearrange("l h -> (l h)")
                                 .partition_broadcast(P)).then_inc(lang_loaded, 16)

            def store(j, b):
                sp.wait_ge(att_added, j * NG + (b + 1) * NG // BT)
                settle(sp, "sp")
                sp.dma_start(out[bass.ds(j * BT + b, 1)].rearrange("b (t p) d -> p (b t) d", p=P),
                             acc[:, 2 * b:2 * b + 2]).then_inc(stored[b], 16)

            def write_parts(k):
                for m in range(4):
                    sp.wait_ge(parts_ready, 4 * k + m + 1)
                    sp.dma_start(scr[m // 2, :, (m % 2) * P:(m % 2 + 1) * P, :].rearrange("s p t -> p s t"),
                                 qk_parts[:, :, m, :]).then_inc(scr_written, 16)

            def read_parts(k):
                sp.wait_ge(scr_written, 64 * (k + 1))
                for b in range(BT):
                    for i, (dst, part) in enumerate(((qs, Q_PART), (ks, K_PART))):
                        for c in range(8):
                            sp.dma_start(dst[16 * c:16 * c + 16, :, b * S:(b + 1) * S],
                                         scr[i, part[c], :, b * S:(b + 1) * S].rearrange("(h d) t -> d h t", d=HD))\
                                .then_inc(qk_loaded[b], 16)

            languages(0)
            write_parts(0)
            sp.wait_ge(wex_ready, 1)
            read_parts(0)
            with sp.Fori(1, STEPS) as k:
                languages(k)
                store(k - 1, 0)
                write_parts(k)
                store(k - 1, 1)
                read_parts(k)
            store(STEPS - 1, 0)
            store(STEPS - 1, 1)
            for b in range(BT):
                sp.wait_ge(stored[b], 16 * STEPS)

        @block.gpsimd
        def _(pool):
            nc.gpsimd.memset(ident[:], 0.0).then_inc(p_step, 1)
            nc.gpsimd.memset(bex_raw[:], 0.0).then_inc(bex_zeroed, 1)
            pool.wait_ge(p_step, 1)
            nc.gpsimd.affine_select(out=ident[:], in_=ident[:], compare_op=ALU.not_equal, fill=1.0, base=0,
                                    pattern=[[-1, P]], channel_multiplier=1).then_inc(ident_made, 1)
            for e in range(E):
                nc.gpsimd.memset(rank_row[:, e:e + 1], float(E - e))
            nc.gpsimd.memset(val[:], 0.0).then_inc(p_step, 1)
            pool.wait_ge(p_step, 2)
            nc.gpsimd.memset(val[:, :, 0:H * VW].rearrange("p t (h w) -> p t h w", w=VW)[:, :, :, HD:VW], 1.0)
            nc.gpsimd.memset(cs[:].bitcast(F32), 0.0).then_inc(consts_made, 1)
            for i in range(2):
                pool.wait_ge(amax_part, i + 1)
                nc.gpsimd.partition_all_reduce(amax[:, 2 + i:3 + i], amax[:, i:i + 1], P,
                                               bass.bass_isa.ReduceOp.max).then_inc(amax_all, 1)
            pool.wait_ge(z_made, 1)
            pool.wait_ge(bias_loaded, 16 * 3)

            xi = x[:, :, 1:D + 1]
            N_STEP = 1

            def main(k):
                base = 2 + k * N_STEP
                n = [0]

                def link(ins):
                    n[0] += 1
                    ins.then_inc(p_step, 1)
                    pool.wait_ge(p_step, base + n[0])
                    settle(pool, "pool")

                if not (isinstance(k, int) and k == 0):
                    xs = a["x"][bass.ds(k * BT, BT)]
                    pool.wait_ge(x1_ready, k * NT)
                    settle(pool, "pool")
                    load_x(pool, xs, x_loaded)
                    pool.wait_ge(at_ready, k * 3 * DC)
                    settle(pool, "pool")
                    load_rows(pool, xs, x_loaded)
                nc.gpsimd.tensor_copy(z_cur[:], z_all[:, :, bass.ds(k * BT, BT)])
                if isinstance(k, int) and k == 0:
                    pool.wait_ge(first_x_loaded, 16 * 14)
                else:
                    pool.wait_ge(x_loaded, 16 * 14 * k)
                settle(pool, "pool")
                nc.gpsimd.tensor_copy(x[:, :, 0:1], x[:, :, 2:3])
                link(nc.gpsimd.tensor_copy(x[:, :, D + 1:D + 2], x[:, :, D - 1:D]))
                nc.gpsimd.tensor_tensor(dn[:], up[:], dn[:], ALU.add)
                wait(pool, parts_ready, k * 4)
                nc.gpsimd.tensor_tensor(lap[:], x[:, :, 0:D], x[:, :, 2:D + 2], ALU.add).then_inc(sums_ready, 1)
                pool.wait_ge(w_ready, k + 1)
                nc.gpsimd.tensor_tensor(up[:], up[:], xi, ALU.mult).then_inc(wx_ready, 1)
                nc.gpsimd.tensor_tensor(xi, xi, bpj_bc[:].unsqueeze(1).to_broadcast([P, NT, D]), ALU.add)\
                    .then_inc(xb_ready, 1)
                pool.wait_ge(lang_loaded, 16 * 18 * (k + 1))
                for t in range(NT):
                    pool.wait_ge(x1_ready, k * NT + t + 1)
                    nc.gpsimd.tensor_tensor(xb2[:, t], x1[:, t], b2_bc[:, t // 2], ALU.add).then_inc(xb2_ready, 1)
                assert n[0] == N_STEP, n[0]

            main(0)
            pool.wait_ge(hi_ready, 12)
            nc.gpsimd.tensor_tensor(wex_l[:], wex_n[:], wex_h[:].bitcast(F32), ALU.subtract).then_inc(wex_ready, 1)
            with pool.Fori(1, STEPS) as k:
                main(k)

        @block.tensor
        def _(pe):
            def mm(o, l, r, start=True, stop=True):
                return pe.matmul(o, l, r, start=start, stop=stop)

            def mm3(o, lh, ll, rh, rl, start, stop):
                mm(o, lh, rh, start, False)
                mm(o, lh, rl, False, False)
                return mm(o, ll, rh, False, stop)

            pe.wait_ge(ident_made, 1)
            pe.wait_ge(lora_loaded, 16 * 6)
            for half in range(2):
                for i in range(4):
                    ins = pe.transpose(banks[half][0:R, i * P:(i + 1) * P], b_fcn[:, 4 * half + i], ident[:])
                ins.then_inc(setup_pe, 1)
            for c in range(DC):
                ins = pe.transpose(banks[2][0:R, c * P:(c + 1) * P], b_pjn[:, c], ident[:])
            ins.then_inc(setup_pe, 1)
            pe.transpose(banks[3][:, 0:12], bias_rows[:], ident[0:12, 0:12]).then_inc(setup_pe, 1)
            pe.wait_ge(factors_ready, 4)
            for c in range(DC):
                for half in range(2):
                    mm(banks[4 + 2 * c + half][:], a_fc[:, c * P:(c + 1) * P], bt_fc[:, half * 512:(half + 1) * 512],
                       True, False)
            pe.wait_ge(eff_ready, 1)
            for c in range(DC):
                for half in range(2):
                    for i in range(4):
                        f = 4 * half + i
                        ins = mm(banks[4 + 2 * c + half][:, i * P:(i + 1) * P],
                                 tq1[:, f * D + c * P:f * D + (c + 1) * P], ident[:], False, i == 3)
                    ins.then_inc(setup_pe, 1)
            for f in range(FC):
                mm(banks[f // 2][:, f % 2 * D:(f % 2 + 1) * D], a_pj[:, f * P:(f + 1) * P], bt_pj[:], f % 2 == 0, False)
            pe.wait_ge(eff_ready, 2)
            for f in range(FC):
                for c in range(DC):
                    ins = mm(banks[f // 2][:, f % 2 * D + c * P:f % 2 * D + (c + 1) * P],
                             tq2[:, c * F + f * P:c * F + (f + 1) * P], ident[:], False, f % 2 == 1 and c == DC - 1)
                if f % 2 == 1:
                    ins.then_inc(setup_pe, 1)
            pe.sem_inc(pt_full, PT_CREDIT)
            pe.sem_inc(pv_done, PV_CREDIT)

            def unit(k, u):
                if u in FREE_WORK:
                    return
                kind, i = u
                prev, earlier = before(u)
                done, n, place = DONE[prev]
                if not (earlier and isinstance(k, int) and k == 0):
                    pe.wait_ge(done, (k - 1 if earlier else k) * n + place + 1)
                o = psum(u)
                if kind in ("CT", "XT", "ZT"):
                    src, ready, each = {"CT": (up, c_ready, 1), "XT": (x1, x1_ready, NT), "ZT": (y, z_ready, NT)}[kind]
                    if each == 1:
                        pe.wait_ge(ready, k + 1)
                    for t in range(NT):
                        if each > 1:
                            pe.wait_ge(ready, k * NT + t + 1)
                        ins = pe.transpose(o[:, t * P:(t + 1) * P], src[:, t, i * P:(i + 1) * P], ident[:])
                elif kind == "FC":
                    pe.wait_ge(at_ready, k * 3 * DC + DC)
                    for c in range(DC):
                        w = slice(i * P, (i + 1) * P)
                        ins = mm3(o[:], wfc_h[:, c, w], wfc_l[:, c, w], act_h[:, c], act_l[:, c], c == 0, c == DC - 1)
                elif kind == "PJ":
                    pe.wait_ge(h_ready, (k + 1) * FC)
                    tok = slice(i * P, (i + 1) * P)
                    for f in range(FC):
                        ins = mm3(o[:, 0:D], hid_h[:, f, tok], hid_l[:, f, tok], wpj_h[:, f], wpj_l[:, f],
                                  f == 0, f == FC - 1)
                elif kind == "A1":
                    pe.wait_ge(at_ready, k * 3 * DC + 2 * DC)
                    pe.wait_ge(lang_split, k + 1)
                    for b in range(BT):
                        tok = slice(b * S, (b + 1) * S)
                        for c in range(DC):
                            ins = mm3(o[:, tok], w1_h[:, b, c], w1_l[:, b, c], act_h[:, c, tok], act_l[:, c, tok],
                                      c == 0, c == DC - 1)
                elif kind == "A2":
                    pe.wait_ge(rs_ready, k + 1)
                    tok = slice(i * P, (i + 1) * P)
                    mm(o[:, 0:D], rs[:, tok], w2_h[:, i // 2], True, False)
                    ins = mm(o[:, 0:D], rs[:, tok], w2_l[:, i // 2], False, True)
                elif kind == "LG":
                    pe.wait_ge(at_ready, (k + 1) * 3 * DC)
                    for c in range(DC):
                        ins = mm3(o[0:E, :], wg_h[:, c], wg_l[:, c], act_h[:, c], act_l[:, c], c == 0, c == DC - 1)
                elif kind == "LT":
                    pe.wait_ge(lgt_ready, k + 1)
                    settle(pe, "pe")
                    for t in range(NT):
                        ins = pe.transpose(o[:, t * E:(t + 1) * E], lgt[:, t * P:(t + 1) * P], ident[0:E, 0:E])
                elif kind == "V":
                    pe.wait_ge(at_ready, (k + 1) * 3 * DC)
                    tok = slice(i * P, (i + 1) * P)
                    for c in range(DC):
                        ins = mm3(o[:, 0:D], act_h[:, c, tok], act_l[:, c, tok], wv_h[:, c], wv_l[:, c],
                                  c == 0, c == DC - 1)
                elif kind == "QK":
                    pe.wait_ge(at_ready, (k + 1) * 3 * DC)
                    w = slice(i * P, (i + 1) * P)
                    for c in range(DC):
                        ins = mm3(o[:], wqk_h[:, c, w], wqk_l[:, c, w], act_h[:, c], act_l[:, c], c == 0, c == DC - 1)
                elif kind == "CB":
                    pe.wait_ge(gate_step, GATE_STEPS * (k + 1))
                    settle(pe, "pe")
                    for t in range(NT):
                        ins = pe.transpose(o[0:64, t * P:(t + 1) * P], cs[:, t].bitcast(F32), ident[:])
                elif kind == "MB":
                    pe.wait_ge(combt_ready, k + 1)
                    ins = mm(o[:, 0:D], cbt[:, i * P:(i + 1) * P], bex[:])
                else:
                    t, q = divmod(i, 4)
                    tok, e2 = slice(t * P, (t + 1) * P), slice(2 * q, 2 * q + 2)
                    for c in range(DC):
                        ins = mm3(o[:], act_h[:, c, tok], act_l[:, c, tok],
                                  wex_h[:, c, e2].rearrange("p e f -> p (e f)"),
                                  wex_l[:, c, e2].rearrange("p e f -> p (e f)"), c == 0, c == DC - 1)
                ins.then_inc(gen_full, 1)

            def scores(j, n):
                b, h = divmod(n, H)
                if h == 0:
                    pe.wait_ge(qk_loaded[b], 256 * (j + 1))
                if n < 2:
                    done, each, place = DONE[[u for u in EXPERTS if BANK[u] == n][-1]]
                    pe.wait_ge(done, each * j + place + 1)
                pe.wait_ge(p_ready, j * NH + n - 1 + P_CREDIT)
                for qt in range(2):
                    q0 = b * S + qt * P
                    ins = mm(sc[n % 2][:, qt * S:(qt + 1) * S], qs[:, h, q0:q0 + P], ks[:, h, b * S:(b + 1) * S])
                ins.then_inc(s_ready, 1)

            def turn(j, n):
                pe.wait_ge(p_ready, j * NH + n + 1 + P_CREDIT)
                pe.wait_ge(pts_ready, j * NH + n - 1 + PTS_CREDIT)
                for kt in range(2):
                    for qt in range(2):
                        ins = pe.transpose(pt[n % 2][:, kt * S + qt * P:kt * S + (qt + 1) * P],
                                           prob[:, n % 2, qt, kt * P:(kt + 1) * P], ident[:])
                ins.then_inc(pt_full, 1)

            def values(j, n):
                b, h = divmod(n, H)
                g, q = divmod(n, 4)
                pe.wait_ge(pts_ready, j * NH + n + 1 + PTS_CREDIT)
                if q == 0:
                    pe.wait_ge(ot_used, j * NG + g - 1 + OT_CREDIT)
                for kt in range(2):
                    ins = mm(ov[g % 2][32 * q:32 * q + 32, 0:S], val[:, 2 * b + kt, h * VW:h * VW + 32],
                             pts[:, n % 2, kt], kt == 0, kt == 1)
                ins.then_inc(pv_done, 1)

            def turn_back(j, g):
                pe.wait_ge(ovs_ready, j * NG + g + 1)
                for qt in range(2):
                    ins = pe.transpose(ov[g % 2][:, S + qt * P:S + (qt + 1) * P], ovs[:, qt * P:(qt + 1) * P], ident[:])
                ins.then_inc(ot_ready, 1)

            def slots(k, j):
                for n in range(NSLOT):
                    if n < NH:
                        scores(j, n)
                    if 2 <= n < NH + 2:
                        turn(j, n - 2)
                    if 3 <= n < NH + 3:
                        values(j, n - 3)
                    if n >= TURN_BACK and (n - TURN_BACK) % 4 == 0 and (n - TURN_BACK) // 4 < NG:
                        turn_back(j, (n - TURN_BACK) // 4)
                    for step, u in shade(k, j, n):
                        unit(step, u)

            for u in SLOTTED + EXPERTS:
                if u in WEIGHTS_FOR:
                    pe.wait_ge(lo_ready, WEIGHTS_FOR[u])
                if u == ("ME", 0):
                    pe.wait_ge(wex_ready, 1)
                unit(0, u)
            with pe.Fori(1, STEPS) as k:
                slots(k, k - 1)
                for u in EXPERTS:
                    unit(k, u)
            slots(None, STEPS - 1)

        @block.scalar
        def _(act):
            def unit(k, u):
                kind, i = u
                if kind == "W":
                    act.wait_ge(sums_ready, k + 1)
                    for b in range(BT):
                        ins = nc.scalar.activation(up[:, 2 * b:2 * b + 2], x[:, 2 * b:2 * b + 2, 1:D + 1], ACT.Identity,
                                                   scale=z_cur[:, 2, b:b + 1], bias=z_cur[:, 3, b:b + 1])
                    ins.then_inc(w_ready, 1)
                elif kind == "ZT":
                    full(act, k, u)
                    for b in range(BT):
                        tok = slice(b * S, (b + 1) * S)
                        ins = nc.scalar.activation(zt[:, i, tok], psum(u)[:, tok], ACT.Identity,
                                                   scale=gb[:, b, 0, i:i + 1], bias=gb[:, b, 1, i:i + 1])
                    ins.then_inc(ah_ready, 1)
                elif kind in ("CT", "XT"):
                    full(act, k, u)
                    nc.scalar.activation(act_h[:, i], psum(u)[:], ACT.Copy).then_inc(ah_ready, 1)
                elif kind == "FC":
                    full(act, k, u)
                    wait(act, h_ready, k * FC + i - 1)
                    signal(nc.scalar.activation(gel[:, i % 2], psum(u)[:], ACT.Gelu, bias=bias_cols[:, i:i + 1]), u)
                elif kind == "A1":
                    full(act, k, u)
                    act.wait_ge(lang_loaded, 16 * 18 * (k + 1))
                    for b in range(BT):
                        tok = slice(b * S, (b + 1) * S)
                        ins = nc.scalar.activation(r1[:, tok], psum(u)[:, tok], ACT.Relu, bias=b1c[:, b:b + 1])
                    signal(ins, u)
                elif kind == "QK":
                    full(act, k, u)
                    nc.scalar.activation(qk_parts[:, 0, i], psum(u)[:], ACT.Identity, bias=bias_cols[:, 8 + i:9 + i])\
                        .then_inc(qk_high_ready, 1)
                elif kind == "LG":
                    full(act, k, u)
                    signal(nc.scalar.activation(lgt[:], psum(u)[0:E, :], ACT.Identity, bias=bg_col[:, 0:1]), u)
                elif kind == "EXP":
                    act.wait_ge(lg_ready, k + 1)
                    nc.scalar.activation(ge[:], lg[:], ACT.Exp).then_inc(ge_ready, 1)
                elif kind == "CB":
                    full(act, k, u)
                    signal(nc.scalar.activation(cbt[:], psum(u)[0:64, :], ACT.Copy), u)

            def exps(j, n):
                act.wait_ge(nm_ready, j * NH + n + 1)
                act.wait_ge(pt_full, j * NH + n - 1 + PT_CREDIT)
                for qt in range(2):
                    ins = nc.scalar.activation(prob[:, n % 2, qt], sc[n % 2][:, qt * S:(qt + 1) * S], ACT.Exp,
                                               bias=nm[:, n % 4, qt:qt + 1])
                ins.then_inc(p_ready, 1)

            def copy_turned(j, n):
                act.wait_ge(pt_full, j * NH + n + 1 + PT_CREDIT)
                act.wait_ge(pv_done, j * NH + n - 1 + PV_CREDIT)
                nc.scalar.activation(pts[:, n % 2].rearrange("p a b -> p (a b)"), pt[n % 2][:], ACT.Copy)\
                    .then_inc(pts_ready, 1)

            def copy_outputs(j, g):
                act.wait_ge(pv_done, j * NH + 4 * g + 4 + PV_CREDIT)
                nc.scalar.activation(ovs[:], ov[g % 2][:, 0:S], ACT.Copy).then_inc(ovs_ready, 1)

            def slots(k, j):
                for n in range(NSLOT):
                    if n >= 7 and n % 4 == 3 and n < 7 + NH:
                        copy_outputs(j, (n - 7) // 4)
                    if 2 <= n < NH + 2:
                        copy_turned(j, n - 2)
                    if n < NH:
                        exps(j, n)
                    for step, u in shade(k, j, n, LAG_ACT):
                        unit(step, u)

            for half in range(2):
                act.wait_ge(setup_pe, half + 1)
                nc.scalar.activation(bt_fc[:, half * 512:(half + 1) * 512], banks[half][0:R, :], ACT.Copy, scale=2.0)\
                    .then_inc(factors_ready, 1)
            act.wait_ge(setup_pe, 3)
            nc.scalar.activation(bt_pj[:], banks[2][0:R, 0:D], ACT.Copy, scale=2.0).then_inc(factors_ready, 1)
            act.wait_ge(setup_pe, 4)
            nc.scalar.activation(bias_cols[:, 0:8], banks[3][:, 0:8], ACT.Copy)
            nc.scalar.activation(bias_cols[:, 8:10], banks[3][:, 8:10], ACT.Copy, scale=0.25)
            nc.scalar.activation(bias_cols[:, 10:12], banks[3][:, 10:12], ACT.Copy).then_inc(factors_ready, 1)

            def hi(dst, src):
                nc.scalar.activation(dst, src, ACT.Copy).then_inc(hi_ready, 1)

            unit(0, ("W", 0))
            for i in range(4):
                act.wait_ge(setup_pe, 4 + i + 1)
                hi(wfc_h[:, i // 2, i % 2 * 512:(i % 2 + 1) * 512], banks[4 + i][:])
            for i in range(4):
                act.wait_ge(setup_pe, 8 + i + 1)
                hi(wpj_h[:, 2 * i:2 * i + 2], banks[i][:].rearrange("p (f o) -> p f o", f=2))
            act.sem_inc(p_ready, P_CREDIT)
            act.sem_inc(pts_ready, PTS_CREDIT)
            for u in SLOTTED[1:] + EXPERTS:
                unit(0, u)
                if u == ("FC", FC - 1):
                    act.wait_ge(rest_loaded, 64)
                    act.wait_ge(bias_loaded, 16 * 3)
                    nc.scalar.activation(wqk_h[:, :, 0:D], wqkv_n[:, :, 0:D], ACT.Copy, scale=0.25)
                    hi(wqk_h[:, :, D:2 * D], wqkv_n[:, :, D:2 * D])
                    hi(wv_h[:], wqkv_n[:, :, 2 * D:3 * D])
                    hi(wg_h[:], wg_n[:])
                    hi(wex_h[:], wex_n[:])
            with act.Fori(1, STEPS) as k:
                slots(k, k - 1)
                for u in EXPERTS:
                    unit(k, u)
            slots(None, STEPS - 1)

        @block.vector
        def _(dve):
            n0 = [0]

            def link0(ins):
                n0[0] += 1
                ins.then_inc(v_step, 1)
                dve.wait_ge(v_step, n0[0])

            for i, (w, q) in enumerate(((wfc_n, tq1), (wpj_n, tq2))):
                dve.wait_ge(w_loaded[i], 16)
                nc.vector.tensor_reduce(amax[:, i:i + 1], w[:].rearrange("p c d -> p (c d)"), AX.X, ALU.max,
                                        apply_absolute_value=True).then_inc(amax_part, 1)
                if i == 1:
                    dve.wait_ge(z_loaded, 16 * 3)
                    link0(nc.vector.tensor_tensor(z_all[:, 3], z_all[:, 0], z_all[:, 1], ALU.add))
                    link0(nc.vector.scalar_tensor_tensor(z_all[:, 3], z_all[:, 3], -2.0, z_all[:, 2],
                                                         ALU.mult, ALU.add))
                    nc.vector.tensor_scalar(z_all[:, 2], z_all[:, 2], -1.0, None, ALU.mult).then_inc(z_made, 1)
                dve.wait_ge(amax_all, i + 1)
                m = amax[:, 2 + i:3 + i]
                link0(nc.vector.tensor_scalar(m, m, 1.0 / QMAX, None, ALU.mult))
                link0(nc.vector.reciprocal(amax[:, i:i + 1], m))
                wf = w[:].rearrange("p c d -> p (c d)")
                link0(nc.vector.tensor_scalar(q[:], wf, amax[:, i:i + 1], MAGIC, ALU.mult, ALU.add))
                link0(nc.vector.tensor_scalar(q[:], q[:], MAGIC, QMIN, ALU.subtract, ALU.max))
                link0(nc.vector.tensor_scalar(q[:], q[:], QMAX, m, ALU.min, ALU.mult))
                link0(nc.vector.tensor_tensor(q[:], q[:], wf, ALU.subtract))
                nc.vector.tensor_tensor(q[:], q[:], wf, ALU.add).then_inc(eff_ready, 1)
            dve.wait_ge(consts_made, 1)
            dve.sem_inc(ot_used, OT_CREDIT)

            def low_part(i):
                dve.wait_ge(hi_ready, i + 1)
                if i < 4:
                    c, w = i // 2, slice(i % 2 * 512, (i % 2 + 1) * 512)
                    ins = nc.vector.tensor_tensor(wfc_l[:, c, w], banks[4 + i][:], wfc_h[:, c, w].bitcast(F32),
                                                  ALU.subtract)
                else:
                    f = slice(2 * (i - 4), 2 * (i - 4) + 2)
                    ins = nc.vector.tensor_tensor(wpj_l[:, f], banks[i - 4][:].rearrange("p (f o) -> p f o", f=2),
                                                  wpj_h[:, f].bitcast(F32), ALU.subtract)
                ins.then_inc(lo_ready, 1)

            def other_weights(part):
                if part == 0:
                    dve.wait_ge(hi_ready, 11)
                    nc.vector.scalar_tensor_tensor(wqk_l[:, :, 0:D], wqkv_n[:, :, 0:D], 0.25,
                                                   wqk_h[:, :, 0:D].bitcast(F32), ALU.mult, ALU.subtract)
                    for low, src, high in ((wqk_l[:, :, D:2 * D], wqkv_n[:, :, D:2 * D], wqk_h[:, :, D:2 * D]),
                                           (wv_l[:], wqkv_n[:, :, 2 * D:3 * D], wv_h[:]),
                                           (wg_l[:], wg_n[:], wg_h[:])):
                        nc.vector.tensor_tensor(low, src, high.bitcast(F32), ALU.subtract).then_inc(lo_ready, 1)
                else:
                    dve.wait_ge(bex_loaded, 64)
                    link0(nc.vector.tensor_copy(bex[:], bex_raw[:]))
                    nc.vector.tensor_tensor(bex[32:64], bex_raw[32:64], bex[32:64].bitcast(F32), ALU.subtract)\
                        .then_inc(lo_ready, 1)


            M_FIRST, M_STEP = 33, 41
            m, m_base = [0], [0]

            def link(ins):
                m[0] += 1
                ins.then_inc(main_step, 1)
                dve.wait_ge(main_step, m_base[0] + m[0])

            def unit(k, u):
                kind, i = u
                o = None if u in FREE_WORK else psum(u)
                if kind == "ST":
                    dve.wait_ge(wx_ready, k + 1)
                    for b in range(BT):
                        ts = slice(2 * b, 2 * b + 2)
                        ins = nc.vector.scalar_tensor_tensor(up[:, ts], (lap, dn)[i][:, ts], z_cur[:, i, b:b + 1],
                                                             up[:, ts], ALU.mult, ALU.add)
                    if i == 0:
                        link(ins)
                    else:
                        ins.then_inc(c_ready, 1)
                elif kind == "SPLIT":
                    split_languages(k)
                elif kind == "LN":
                    normalize(k, i)
                elif kind == "LT":
                    full(dve, k, u)
                    signal(nc.vector.tensor_copy(lg[:], o[:, 0:NT * E].rearrange("p (t e) -> p t e", e=E)), u)
                    dve.wait_ge(logits_made, k + 1)
                    gate_shift()
                elif kind == "ZT":
                    dve.wait_ge(ah_ready, DONE[u][1] * k + DONE[u][2] + 1)
                    link(nc.vector.tensor_copy(act_h[:, i], zt[:, i]))
                    signal(nc.vector.tensor_tensor(act_l[:, i], zt[:, i], act_h[:, i].bitcast(F32), ALU.subtract), u)
                elif kind in ("CT", "XT"):
                    dve.wait_ge(ah_ready, DONE[u][1] * k + DONE[u][2] + 1)
                    signal(nc.vector.tensor_tensor(act_l[:, i], o[:], act_h[:, i].bitcast(F32), ALU.subtract), u)
                elif kind == "FC":
                    dve.wait_ge(g_ready, k * FC + i + 1)
                    link(nc.vector.tensor_copy(hid_h[:, i], gel[:, i % 2]))
                    nc.vector.tensor_tensor(hid_l[:, i], gel[:, i % 2], hid_h[:, i].bitcast(F32), ALU.subtract)\
                        .then_inc(h_ready, 1)
                elif kind == "PJ":
                    full(dve, k, u)
                    dve.wait_ge(xb_ready, k + 1)
                    signal(nc.vector.tensor_tensor(x1[:, i], o[:, 0:D], x[:, i, 1:D + 1], ALU.add), u)
                elif kind == "A1":
                    dve.wait_ge(r1_ready, k + 1)
                    link(nc.vector.tensor_copy(rs[:], r1[:]))
                    nc.vector.tensor_tensor(rs[A:P], r1[A:P], rs[A:P].bitcast(F32), ALU.subtract).then_inc(rs_ready, 1)
                elif kind == "A2":
                    full(dve, k, u)
                    dve.wait_ge(xb2_ready, k * NT + i + 1)
                    signal(nc.vector.tensor_tensor(y[:, i], o[:, 0:D], xb2[:, i], ALU.add), u)
                    if i >= 1:
                        stats(k, i - 1)
                    if i >= 2:
                        moments(k, i - 2)
                elif kind == "V":
                    full(dve, k, u)
                    signal(nc.vector.tensor_tensor(val[:, i, 0:H * VW].rearrange("p (h w) -> p h w", w=VW)[:, :, 0:HD],
                                                   o[:, 0:D].rearrange("p (h d) -> p h d", d=HD),
                                                   bv_bc[:].rearrange("p (h d) -> p h d", d=HD), ALU.add), u)
                    gate_steps(k, *GATE_AT.get(u, ()))
                elif kind == "QK":
                    dve.wait_ge(qk_high_ready, 4 * k + i + 1)
                    q = qf[:, i % 2]
                    signal(nc.vector.scalar_tensor_tensor(q, o[:], bias_cols[:, 8 + i:9 + i], qk_parts[:, 0, i],
                                                          ALU.add, ALU.subtract), u)
                    first, second, third = GATE_AT[u]
                    gate_steps(k, *first)
                    dve.wait_ge(qf_ready, 4 * k + i + 1)
                    nc.vector.tensor_copy(qk_parts[:, 1, i], q).then_inc(qk_mid_ready, 1)
                    gate_steps(k, *second)
                    dve.wait_ge(qk_mid_ready, 4 * k + i + 1)
                    nc.vector.tensor_tensor(qk_parts[:, 2, i], q, qk_parts[:, 1, i], ALU.subtract)\
                        .then_inc(parts_ready, 1)
                    gate_steps(k, *third)
                elif kind == "MB":
                    full(dve, k, u)
                    late = i >= NT // BT
                    if late:
                        wait(dve, stored[i // 2], 16 * k)
                    else:
                        dve.wait_ge(moe_added, DONE[u][1] * k + DONE[u][2] - 1)
                    signal(nc.vector.tensor_tensor(acc[:, i], o[:, 0:D], x1[:, i] if late else acc[:, i], ALU.add), u)
                elif kind == "ME":
                    t, q = divmod(i, 4)
                    if u in LATE_EXPERTS:
                        experts(k, [u], q)
                    elif t % 2 == 1:
                        experts(k, [("ME", i - 4), u], q)

            def experts(k, pair, q):
                early = pair[0] in EXPERTS
                for u in pair:
                    full(dve, k, u)
                    if q == 0 and early:
                        dve.wait_ge(gate_step, GATE_STEPS * (k + 1))
                        wait(dve, stored[0], 16 * k)
                    elif q == 0:
                        dve.wait_ge(moe_added, DONE[pair[0]][1] * k + DONE[pair[0]][2])
                    else:
                        dve.wait_ge(moe_added, DONE[u][1] * k + DONE[u][2] - 1)
                    t = u[1] // 4
                    nc.vector.scalar_tensor_tensor(acc[:, t], psum(u)[:, 0:D], cmb[:, t, 2 * q:2 * q + 1],
                                                   x1[:, t] if early and q == 0 else acc[:, t], ALU.mult, ALU.add)\
                        .then_inc(main_step, 1)
                for n, u in enumerate(pair):
                    t = u[1] // 4
                    m[0] += 1
                    dve.wait_ge(main_step, m_base[0] + m[0])
                    signal(nc.vector.scalar_tensor_tensor(acc[:, t], psum(u)[:, D:2 * D],
                                                          cmb[:, t, 2 * q + 1:2 * q + 2], acc[:, t],
                                                          ALU.mult, ALU.add), u)

            def wide(v):
                return v.unsqueeze(2).to_broadcast([P, NT, E])

            def gate_shift():
                link(nc.vector.tensor_reduce(gm[:], lg[:], AX.X, ALU.max))
                nc.vector.tensor_tensor(lg[:], lg[:], wide(gm[:]), ALU.subtract).then_inc(lg_ready, 1)

            def gate_steps(k, *at):
                for i in at:
                    if i == 0:
                        dve.wait_ge(ge_ready, k + 1)
                    else:
                        dve.wait_ge(gate_step, GATE_STEPS * k + i)
                    gate(i).then_inc(gate_step, 1)

            def gate(i):
                if i == 0:
                    return nc.vector.tensor_reduce(gm[:], ge[:], AX.X, ALU.add)
                if i == 1:
                    return nc.vector.reciprocal(gm[:], gm[:])
                if i == 2:
                    return nc.vector.tensor_tensor(gt[:], ge[:], wide(gm[:]), ALU.mult)
                g, s, top = (gt, s1, i - 3) if i < 9 else (g2, s2, i - 9)
                if top == 0:
                    return nc.vector.tensor_reduce(gm[:], g[:], AX.X, ALU.max)
                if top == 1:
                    return nc.vector.tensor_tensor(eq[:], g[:], wide(gm[:]), ALU.is_equal)
                if top == 2:
                    return nc.vector.tensor_tensor(eq[:], eq[:], rank_row[:].unsqueeze(1).to_broadcast([P, NT, E]),
                                                   ALU.mult)
                if top == 3:
                    return nc.vector.tensor_reduce(gm[:], eq[:], AX.X, ALU.max)
                if top == 4:
                    return nc.vector.tensor_tensor(s[:], eq[:], wide(gm[:]), ALU.is_equal)
                if i == 8:
                    return nc.vector.scalar_tensor_tensor(g2[:], s1[:], -2.0, gt[:], ALU.mult, ALU.add)
                if i == 14:
                    return nc.vector.tensor_tensor(s1[:], s1[:], s2[:], ALU.add)
                if i == 15:
                    return nc.vector.tensor_tensor(cmb[:], s1[:], gt[:], ALU.mult)
                if i < 18:
                    at = (0, 32)[i - 16]
                    return nc.vector.tensor_copy(cs[:, :, at:at + E], cmb[:])
                at = (E, 32 + E)[i - 18]
                return nc.vector.tensor_tensor(cs[:, :, at:at + E], cmb[:], cs[:, :, 0:E].bitcast(F32), ALU.subtract)

            def split_languages(k):
                dve.wait_ge(lang_loaded, 16 * 18 * (k + 1))
                w1 = wraw[:, 0].rearrange("p b (c m) -> p b c m", c=DC)
                nc.vector.tensor_copy(w1_h[:], w1)
                link(nc.vector.tensor_copy(w2_h[:], wraw[:, 1]))
                nc.vector.tensor_tensor(w1_l[:], w1, w1_h[:].bitcast(F32), ALU.subtract)
                nc.vector.tensor_tensor(w2_l[:], wraw[:, 1], w2_h[:].bitcast(F32), ALU.subtract).then_inc(lang_split, 1)

            def stats(k, t):
                dve.wait_ge(y_ready, k * NT + t + 1)
                nc.vector.bn_stats(st[:, t], y[:, t]).then_inc(st_ready, 1)

            def moments(k, t):
                dve.wait_ge(st_ready, k * NT + t + 1)
                settle(dve, "dve")
                nc.vector.bn_aggr(mv[:, t], st[:, t]).then_inc(mv_ready, 1)

            def normalize(k, i):
                if i == 0:
                    stats(k, NT - 1)
                    moments(k, NT - 2)
                    moments(k, NT - 1)
                    dve.wait_ge(mv_ready, (k + 1) * NT)
                    link(nc.vector.tensor_scalar(ve[:], mv[:, :, 1], LN_EPS, None, ALU.add))
                    link(nc.vector.tensor_scalar(rsd[:].bitcast(I32), ve[:].bitcast(I32), -0.5, RSQRT_SEED,
                                                 ALU.mult, ALU.add))
                elif i <= NEWTON:
                    link(nc.vector.scalar_tensor_tensor(rst[:], rsd[:], -0.5, rsd[:], ALU.mult, ALU.mult))
                    link(nc.vector.tensor_tensor(rst[:], rst[:], ve[:], ALU.mult))
                    link(nc.vector.scalar_tensor_tensor(rsd[:], rst[:], 1.5, rsd[:], ALU.add, ALU.mult))
                else:
                    for t in range(NT):
                        nc.vector.tensor_scalar(y[:, t], y[:, t], mv[:, t, 0:1], rsd[:, t:t + 1], ALU.subtract,
                                                ALU.mult).then_inc(z_ready, 1)

            s = [0]

            def alink(j, ins):
                s[0] += 1
                ins.then_inc(att_step, 1)
                dve.wait_ge(att_step, j * NG + s[0])

            def slots(k, j):
                s[0] = 0
                for n in range(NSLOT):
                    if n < NH:
                        dve.wait_ge(s_ready, j * NH + n + 1)
                        nc.vector.tensor_reduce(nm[:, n % 4], sc[n % 2][:].rearrange("p (q k) -> p q k", q=2), AX.X,
                                                ALU.max, negate=True).then_inc(nm_ready, 1)
                    if n >= NORM and (n - NORM) % 4 == 0:
                        g = (n - NORM) // 4
                        b, gb = divmod(g, NG // BT)
                        dve.wait_ge(ot_ready, j * NG + g + 1)
                        o = ov[g % 2][:, S:2 * S].rearrange("p (q h w) -> p q h w", q=2, h=4)
                        alink(j, nc.vector.reciprocal(rden[:], o[:, :, :, HD:VW]))
                        nc.vector.tensor_tensor(tmp[:], o[:, :, :, 0:HD], rden[:].to_broadcast([P, 2, 4, HD]),
                                                ALU.mult).then_inc(ot_used, 1)
                        dve.wait_ge(ot_used, j * NG + g + 1 + OT_CREDIT)
                        dst = acc[:, 2 * b:2 * b + 2, gb * 4 * HD:(gb + 1) * 4 * HD]
                        nc.vector.tensor_tensor(dst, dst, tmp[:].rearrange("p q h w -> p q (h w)"), ALU.add)\
                            .then_inc(att_added, 1)
                    for step, u in shade(k, j, n, LAG_DVE):
                        unit(step, u)

            for i in range(4):
                low_part(i)
            for u in SLOTTED + EXPERTS:
                unit(0, u)
                if u == ("CT", 1):
                    for i in range(4, 8):
                        low_part(i)
                elif u == ("PJ", 0):
                    other_weights(0)
                elif u == ("PJ", 3):
                    other_weights(1)
            assert m[0] == M_FIRST, f"{m[0]} steps"
            with dve.Fori(1, STEPS) as k:
                m[0], m_base[0] = 0, (k - 1) * M_STEP + M_FIRST
                slots(k, k - 1)
                for u in EXPERTS:
                    unit(k, u)
                assert m[0] == M_STEP, f"{m[0]} steps"
            m[0], m_base[0] = 0, (STEPS - 1) * M_STEP + M_FIRST
            slots(None, STEPS - 1)


_INS = ["x", "condB_zX", "condB_zY", "condB_zR", "itok_B_0_8", "L0_ffn_W_fc", "L0_ffn_b_fc", "L0_ffn_A_fc",
        "L0_ffn_B_fc", "L0_ffn_W_proj", "L0_ffn_b_proj", "L0_ffn_A_proj", "L0_ffn_B_proj", "L1_cond_W1",
        "L1_cond_b1", "L1_cond_W2", "L1_cond_b2", "L1_cond_gamma", "L1_cond_beta", "L1_ffn_W_qkv",
        "L1_ffn_b_qkv", "L1_ffn_W_gate", "L1_ffn_b_gate", "L1_ffn_W_experts", "L1_ffn_b_experts"]


def kernel(**inputs):
    import numpy as np
    import concourse.bacc as bacc
    from concourse.bass_utils import run_bass_kernel_spmd

    nc = bacc.Bacc("TRN2", target_bir_lowering=False, num_devices=1)
    arrays, aps = {}, {}
    for name in _INS:
        v = np.ascontiguousarray(inputs[name])
        arrays[f"in_{name}"] = v
        aps[name] = nc.dram_tensor(f"in_{name}", v.shape, mybir.dt.from_np(v.dtype), kind="ExternalInput").ap()
    out = nc.dram_tensor("out", (B, S, D), F32, kind="ExternalOutput").ap()
    block_kernel(nc, aps, out)
    return run_bass_kernel_spmd(nc, [arrays], core_ids=[0]).results[0]["out"]
```
